# Optimizing a Trainium2 kernel written in Bass

```python
import numpy as np
import jax
import jax.numpy as jnp

def _softmax(x, axis=-1):
    return jax.nn.softmax(x, axis=axis)

def _gelu(x):
    return jax.nn.gelu(x, approximate=True)

def _silu(x):
    return jax.nn.silu(x)

def _sigmoid(x):
    return jax.nn.sigmoid(x)

def _layernorm(x, axis=-1, eps=1e-05):
    m = jnp.mean(x, axis=axis, keepdims=True)
    v = jnp.var(x, axis=axis, keepdims=True)
    return (x - m) / jnp.sqrt(v + eps)

def _scatter_add(tgt, idx, src, axis=0):
    return tgt.at[idx].add(src)

def _segment_sum(src, seg, n):
    return jax.ops.segment_sum(src, seg, n)
kernel_name = 'mk_gnn_resnorm_d2_gnn_r8_060ef3'

def setup_inputs(seed: int=0):
    np.random.seed(seed)
    _w = jnp.asarray

    def _rec_inputs():
        import jax
        import jax.numpy as jnp
        _gk = jax.random.key(seed)
        x = -0.0005121 + 1.001 * jax.random.normal(jax.random.fold_in(_gk, 1), (12500, 160), jnp.float32)
        src = jax.random.randint(jax.random.fold_in(_gk, 2), (200000,), 0, 12500, jnp.int32)
        dst = jnp.minimum((12500 * jax.random.uniform(jax.random.fold_in(_gk, 3), (200000,)) ** 2.0).astype(jnp.int32), 99999)
        _o = jnp.argsort(dst, stable=True)
        src = src[_o]
        dst = dst[_o]
        edge_attr_16 = -0.000191324 + 0.999809 * jax.random.normal(jax.random.fold_in(_gk, 12), (200000, 16), jnp.float32)
        edge_attr_4 = 0.000126197 + 0.999763 * jax.random.normal(jax.random.fold_in(_gk, 13), (200000, 4), jnp.float32)
        node_vec1 = jax.random.uniform(jax.random.fold_in(_gk, 15), (12500, 1), jnp.float32, 0.0, 1)
        return (x, src, dst, edge_attr_16, edge_attr_4, node_vec1)
    x, src, dst, edge_attr_16, edge_attr_4, node_vec1 = _rec_inputs()

    def _L0_gnn_setup():
        import jax, jax.numpy as jnp
        import numpy as np
        N = 2500
        E = 40000
        MUL0 = 64
        MUL1 = 32
        FC_IN = 16
        FC_H = 64
        WNUM = 192
        key = jax.random.key(seed)
        ks = jax.random.split(key, 16)
        return {'x': jax.random.normal(ks[0], (N, MUL0 + 3 * MUL1), jnp.float32), 'node_attr': jnp.ones((N, 1), jnp.float32), 'edge_scalars': jax.random.normal(ks[1], (E, FC_IN), jnp.float32), 'edge_attr_sh': jax.random.normal(ks[2], (E, 4), jnp.float32), 'edge_src': jax.random.randint(ks[3], (E,), 0, N), 'edge_dst': jax.random.randint(ks[4], (E,), 0, N), 'Wfc1': jax.random.normal(ks[5], (FC_IN, FC_H), jnp.float32), 'Wfc2': jax.random.normal(ks[6], (FC_H, WNUM), jnp.float32), 'Wsc0': jax.random.normal(ks[7], (MUL0, MUL0), jnp.float32), 'Wsc1': jax.random.normal(ks[8], (MUL1, MUL1), jnp.float32), 'Wl1_0': jax.random.normal(ks[9], (MUL0, MUL0), jnp.float32), 'Wl1_1': jax.random.normal(ks[10], (MUL1, MUL1), jnp.float32), 'Wl2_s': jax.random.normal(ks[11], (MUL0 + MUL1, MUL0), jnp.float32), 'Wl2_v': jax.random.normal(ks[12], (MUL0 + MUL1, MUL1), jnp.float32), 'Wa': 0.1 * jax.random.normal(ks[13], (MUL0 + MUL1, 1), jnp.float32)}
    _L0_gnn_all = _L0_gnn_setup()
    _L0_gnn_in = {k: v for k, v in _L0_gnn_all.items() if k in ('Wfc1', 'Wfc2', 'Wsc0', 'Wsc1', 'Wl1_0', 'Wl1_1', 'Wl2_s', 'Wl2_v', 'Wa')}
    del _L0_gnn_all

    def _L1_gnn_setup():
        import jax, jax.numpy as jnp
        import numpy as np
        N, E = (2500, 40000)
        CS, CV = (64, 32)
        AS_, AV, H = (16, 8, 4)
        NB = 16
        SQRT3 = 1.7320508075688772
        SQRT2 = 1.4142135623730951
        EPS = 1e-05

        def _cg_tp(s, v, y0, y1, w_ss, w_sv, w_vs, w_vv0, w_vv1):
            out_s = jnp.concatenate([w_ss * s * y0[:, None], w_vv0 * (jnp.einsum('eci,ei->ec', v, y1) / SQRT3)], axis=-1)
            out_v = jnp.concatenate([(w_sv * s)[:, :, None] * y1[:, None, :], (w_vs * jnp.ones_like(v[..., 0]))[..., None] * v * y0[:, None, None], (w_vv1 * jnp.ones_like(v[..., 0]))[..., None] * (jnp.cross(v, y1[:, None, :]) / SQRT2)], axis=1)
            return (out_s, out_v)

        def _equiv_layernorm(s, v, gamma_s, beta_s, gamma_v):
            mu = jnp.mean(s, axis=-1, keepdims=True)
            var = jnp.var(s, axis=-1, keepdims=True)
            s_n = (s - mu) * jax.lax.rsqrt(var + EPS) * gamma_s + beta_s
            rms = jnp.sqrt(jnp.mean(jnp.sum(v * v, axis=-1), axis=-1, keepdims=True) + EPS)
            v_n = v / rms[..., None] * gamma_v[None, :, None]
            return (s_n, v_n)
        key = jax.random.key(seed)
        ks = jax.random.split(key, 26)

        def rn(k, shape, fan):
            return jax.random.normal(k, shape, jnp.float32) / np.sqrt(fan)
        D1S, D1V = (CS + CV, CS + 2 * CV)
        WN = 2 * CS + 3 * CV
        inp = {'node': jax.random.normal(ks[0], (N, CS + 3 * CV), jnp.float32), 'edge_index': jax.random.randint(ks[1], (2, E), 0, N, jnp.int64 if jax.config.jax_enable_x64 else jnp.int32), 'rbf': jax.random.uniform(ks[2], (E, NB), jnp.float32), 'rsh': jax.random.normal(ks[3], (E, 4), jnp.float32), 'gamma_s': jnp.ones((CS,), jnp.float32), 'beta_s': jnp.zeros((CS,), jnp.float32), 'gamma_v': jnp.ones((CV,), jnp.float32), 'Ws_src': rn(ks[4], (CS, CS), CS), 'Wv_src': rn(ks[5], (CV, CV), CV), 'Ws_dst': rn(ks[6], (CS, CS), CS), 'Wv_dst': rn(ks[7], (CV, CV), CV), 'W_rbf': rn(ks[8], (NB, WN), NB), 'W_alpha': rn(ks[9], (D1S, H * AS_), D1S), 'alpha_dot': rn(ks[10], (1, H, AS_), AS_), 'Ws_val': rn(ks[11], (D1S, CS), D1S), 'Wv_val': rn(ks[12], (D1V, CV), D1V), 'Wg': rn(ks[13], (CS, CV), CS), 'w2_ss': rn(ks[14], (CS,), 1), 'w2_sv': rn(ks[15], (CS,), 1), 'w2_vs': rn(ks[16], (CV,), 1), 'w2_vv0': rn(ks[17], (CV,), 1), 'w2_vv1': rn(ks[18], (CV,), 1), 'Ws_vlin': rn(ks[19], (D1S, H * AS_), D1S), 'Wv_vlin': rn(ks[20], (D1V, H * AV), D1V), 'Wps': rn(ks[21], (H * AS_, CS), H * AS_), 'Wpv': rn(ks[22], (H * AV, CV), H * AV)}
        return inp
    _L1_gnn_all = _L1_gnn_setup()
    _L1_gnn_in = {k: v for k, v in _L1_gnn_all.items() if k in ('gamma_s', 'beta_s', 'gamma_v', 'Ws_src', 'Wv_src', 'Ws_dst', 'Wv_dst', 'W_rbf', 'W_alpha', 'alpha_dot', 'Ws_val', 'Wv_val', 'Wg', 'w2_ss', 'w2_sv', 'w2_vs', 'w2_vv0', 'w2_vv1', 'Ws_vlin', 'Wv_vlin', 'Wps', 'Wpv')}
    del _L1_gnn_all
    return {'x': x, 'src': src, 'dst': dst, 'edge_attr_16': edge_attr_16, 'edge_attr_4': edge_attr_4, 'node_vec1': node_vec1, 'L0_gnn_Wfc1': _L0_gnn_in['Wfc1'], 'L0_gnn_Wfc2': _L0_gnn_in['Wfc2'], 'L0_gnn_Wsc0': _L0_gnn_in['Wsc0'], 'L0_gnn_Wsc1': _L0_gnn_in['Wsc1'], 'L0_gnn_Wl1_0': _L0_gnn_in['Wl1_0'], 'L0_gnn_Wl1_1': _L0_gnn_in['Wl1_1'], 'L0_gnn_Wl2_s': _L0_gnn_in['Wl2_s'], 'L0_gnn_Wl2_v': _L0_gnn_in['Wl2_v'], 'L0_gnn_Wa': _L0_gnn_in['Wa'], 'L1_gnn_gamma_s': _L1_gnn_in['gamma_s'], 'L1_gnn_beta_s': _L1_gnn_in['beta_s'], 'L1_gnn_gamma_v': _L1_gnn_in['gamma_v'], 'L1_gnn_Ws_src': _L1_gnn_in['Ws_src'], 'L1_gnn_Wv_src': _L1_gnn_in['Wv_src'], 'L1_gnn_Ws_dst': _L1_gnn_in['Ws_dst'], 'L1_gnn_Wv_dst': _L1_gnn_in['Wv_dst'], 'L1_gnn_W_rbf': _L1_gnn_in['W_rbf'], 'L1_gnn_W_alpha': _L1_gnn_in['W_alpha'], 'L1_gnn_alpha_dot': _L1_gnn_in['alpha_dot'], 'L1_gnn_Ws_val': _L1_gnn_in['Ws_val'], 'L1_gnn_Wv_val': _L1_gnn_in['Wv_val'], 'L1_gnn_Wg': _L1_gnn_in['Wg'], 'L1_gnn_w2_ss': _L1_gnn_in['w2_ss'], 'L1_gnn_w2_sv': _L1_gnn_in['w2_sv'], 'L1_gnn_w2_vs': _L1_gnn_in['w2_vs'], 'L1_gnn_w2_vv0': _L1_gnn_in['w2_vv0'], 'L1_gnn_w2_vv1': _L1_gnn_in['w2_vv1'], 'L1_gnn_Ws_vlin': _L1_gnn_in['Ws_vlin'], 'L1_gnn_Wv_vlin': _L1_gnn_in['Wv_vlin'], 'L1_gnn_Wps': _L1_gnn_in['Wps'], 'L1_gnn_Wpv': _L1_gnn_in['Wpv']}

def reference(x, src, dst, edge_attr_16, edge_attr_4, node_vec1, L0_gnn_Wfc1, L0_gnn_Wfc2, L0_gnn_Wsc0, L0_gnn_Wsc1, L0_gnn_Wl1_0, L0_gnn_Wl1_1, L0_gnn_Wl2_s, L0_gnn_Wl2_v, L0_gnn_Wa, L1_gnn_gamma_s, L1_gnn_beta_s, L1_gnn_gamma_v, L1_gnn_Ws_src, L1_gnn_Wv_src, L1_gnn_Ws_dst, L1_gnn_Wv_dst, L1_gnn_W_rbf, L1_gnn_W_alpha, L1_gnn_alpha_dot, L1_gnn_Ws_val, L1_gnn_Wv_val, L1_gnn_Wg, L1_gnn_w2_ss, L1_gnn_w2_sv, L1_gnn_w2_vs, L1_gnn_w2_vv0, L1_gnn_w2_vv1, L1_gnn_Ws_vlin, L1_gnn_Wv_vlin, L1_gnn_Wps, L1_gnn_Wpv):
    import jax
    import jax.numpy as jnp

    def _L0_gnn_ref(x, node_attr, edge_scalars, edge_attr_sh, edge_src, edge_dst, Wfc1, Wfc2, Wsc0, Wsc1, Wl1_0, Wl1_1, Wl2_s, Wl2_v, Wa):
        import jax, jax.numpy as jnp
        import numpy as np
        N = 2500
        E = 40000
        MUL0 = 64
        MUL1 = 32
        FC_IN = 16
        FC_H = 64
        WNUM = 192
        n = x.shape[0]
        x0 = x[:, :MUL0]
        x1 = x[:, MUL0:].reshape(n, MUL1, 3)
        a = node_attr
        h = jax.nn.silu(edge_scalars @ (Wfc1 / jnp.sqrt(jnp.float32(FC_IN))))
        w = h @ (Wfc2 / jnp.sqrt(jnp.float32(FC_H)))
        w0 = w[:, :64]
        w1 = w[:, 64:128]
        w2 = w[:, 128:160]
        w3 = w[:, 160:192]
        inv8 = 1.0 / jnp.sqrt(jnp.float32(MUL0))
        inv32 = 1.0 / jnp.sqrt(jnp.float32(MUL1))
        sc = jnp.concatenate([x0 @ Wsc0 * a * inv8, (jnp.einsum('num,uv->nvm', x1, Wsc1) * a[..., None] * inv32).reshape(n, 3 * MUL1)], axis=1)
        f0 = x0 @ Wl1_0 * a * inv8
        f1 = jnp.einsum('num,uv->nvm', x1, Wl1_1) * a[..., None] * inv32
        e0 = f0[edge_src]
        e1 = f1[edge_src]
        sh0 = edge_attr_sh[:, :1]
        sh1 = edge_attr_sh[:, 1:4]
        mid0 = w0 * e0 * sh0
        mid1 = w3 * jnp.einsum('eum,em->eu', e1, sh1) / jnp.sqrt(3.0)
        mid2 = w1[:, :, None] * e0[:, :, None] * sh1[:, None, :]
        mid3 = w2[:, :, None] * e1 * sh0[:, :, None]
        cnt = jnp.clip(jax.ops.segment_sum(jnp.ones(edge_dst.shape, x.dtype), edge_dst, num_segments=n), 1.0)

        def smean(v):
            s = jax.ops.segment_sum(v, edge_dst, num_segments=n)
            return s / cnt.reshape((n,) + (1,) * (v.ndim - 1))
        n0, n1 = (smean(mid0), smean(mid1))
        n2, n3 = (smean(mid2), smean(mid3))
        scal = jnp.concatenate([n0, n1], axis=1)
        vec = jnp.concatenate([n2, n3], axis=1)
        inv96 = 1.0 / jnp.sqrt(jnp.float32(MUL0 + MUL1))
        alpha = scal @ Wa * a * inv96
        out_s = scal @ Wl2_s * a * inv96
        out_v = jnp.einsum('num,uv->nvm', vec, Wl2_v) * a[..., None] * inv96
        conv = jnp.concatenate([out_s, out_v.reshape(n, 3 * MUL1)], axis=1)
        return sc + alpha * conv

    def _L1_gnn_ref(node, rbf, rsh, gamma_s, beta_s, gamma_v, Ws_src, Wv_src, Ws_dst, Wv_dst, W_rbf, W_alpha, alpha_dot, Ws_val, Wv_val, Wg, w2_ss, w2_sv, w2_vs, w2_vv0, w2_vv1, Ws_vlin, Wv_vlin, Wps, Wpv, edge_index):
        import jax, jax.numpy as jnp
        import numpy as np
        N, E = (2500, 40000)
        CS, CV = (64, 32)
        AS_, AV, H = (16, 8, 4)
        NB = 16
        SQRT3 = 1.7320508075688772
        SQRT2 = 1.4142135623730951
        EPS = 1e-05

        def _cg_tp(s, v, y0, y1, w_ss, w_sv, w_vs, w_vv0, w_vv1):
            out_s = jnp.concatenate([w_ss * s * y0[:, None], w_vv0 * (jnp.einsum('eci,ei->ec', v, y1) / SQRT3)], axis=-1)
            out_v = jnp.concatenate([(w_sv * s)[:, :, None] * y1[:, None, :], (w_vs * jnp.ones_like(v[..., 0]))[..., None] * v * y0[:, None, None], (w_vv1 * jnp.ones_like(v[..., 0]))[..., None] * (jnp.cross(v, y1[:, None, :]) / SQRT2)], axis=1)
            return (out_s, out_v)

        def _equiv_layernorm(s, v, gamma_s, beta_s, gamma_v):
            mu = jnp.mean(s, axis=-1, keepdims=True)
            var = jnp.var(s, axis=-1, keepdims=True)
            s_n = (s - mu) * jax.lax.rsqrt(var + EPS) * gamma_s + beta_s
            rms = jnp.sqrt(jnp.mean(jnp.sum(v * v, axis=-1), axis=-1, keepdims=True) + EPS)
            v_n = v / rms[..., None] * gamma_v[None, :, None]
            return (s_n, v_n)
        n = node.shape[0]
        e = rsh.shape[0]
        s = node[:, :CS]
        v = node[:, CS:].reshape(n, CV, 3)
        s_n, v_n = _equiv_layernorm(s, v, gamma_s, beta_s, gamma_v)
        src, dst = (edge_index[0], edge_index[1])
        msg_s = (s_n @ Ws_src)[src] + (s_n @ Ws_dst)[dst]
        msg_v = jnp.einsum('ncx,cd->ndx', v_n, Wv_src)[src] + jnp.einsum('ncx,cd->ndx', v_n, Wv_dst)[dst]
        y0, y1 = (rsh[:, 0], rsh[:, 1:4])
        w1 = rbf @ W_rbf
        m1_s, m1_v = _cg_tp(msg_s, msg_v, y0, y1, w1[:, :CS], w1[:, CS:2 * CS], w1[:, 2 * CS:2 * CS + CV], w1[:, 2 * CS + CV:2 * CS + 2 * CV], w1[:, 2 * CS + 2 * CV:])
        a = (m1_s @ W_alpha).reshape(e, H, AS_)
        a = jnp.where(a > 0, a, 0.2 * a)
        a = jnp.sum(a * alpha_dot, axis=-1, keepdims=True)
        amax = jax.ops.segment_max(a, dst, num_segments=n)
        amax = jnp.where(jnp.isfinite(amax), amax, 0.0)
        ex = jnp.exp(a - amax[dst])
        den = jax.ops.segment_sum(ex, dst, num_segments=n)
        alpha = ex / (den[dst] + 1e-16)
        val_s = m1_s @ Ws_val
        val_v = jnp.einsum('ecx,cd->edx', m1_v, Wv_val)
        val_v = val_v * jax.nn.sigmoid(val_s @ Wg)[..., None]
        val_s = jax.nn.sigmoid(val_s)
        m2_s, m2_v = _cg_tp(val_s, val_v, y0, y1, w2_ss, w2_sv, w2_vs, w2_vv0, w2_vv1)
        hs = (m2_s @ Ws_vlin).reshape(e, H, AS_)
        hv = jnp.einsum('ecx,cd->edx', m2_v, Wv_vlin).reshape(e, H, AV, 3)
        h = jnp.concatenate([hs, hv.reshape(e, H, AV * 3)], axis=-1)
        agg = jax.ops.segment_sum(alpha * h, dst, num_segments=n)
        agg_s = agg[:, :, :AS_].reshape(n, H * AS_)
        agg_v = agg[:, :, AS_:].reshape(n, H * AV, 3)
        out = node + jnp.concatenate([agg_s @ Wps, jnp.einsum('ncx,cd->ndx', agg_v, Wpv).reshape(n, CV * 3)], axis=-1)
        return out
    edge_index = jnp.stack([src, dst])
    x = _layernorm(x + _L0_gnn_ref(x, node_vec1, edge_attr_16, edge_attr_4, src, dst, L0_gnn_Wfc1, L0_gnn_Wfc2, L0_gnn_Wsc0, L0_gnn_Wsc1, L0_gnn_Wl1_0, L0_gnn_Wl1_1, L0_gnn_Wl2_s, L0_gnn_Wl2_v, L0_gnn_Wa), axis=-1)
    x = _layernorm(x + _L1_gnn_ref(x, edge_attr_16, edge_attr_4, L1_gnn_gamma_s, L1_gnn_beta_s, L1_gnn_gamma_v, L1_gnn_Ws_src, L1_gnn_Wv_src, L1_gnn_Ws_dst, L1_gnn_Wv_dst, L1_gnn_W_rbf, L1_gnn_W_alpha, L1_gnn_alpha_dot, L1_gnn_Ws_val, L1_gnn_Wv_val, L1_gnn_Wg, L1_gnn_w2_ss, L1_gnn_w2_sv, L1_gnn_w2_vs, L1_gnn_w2_vv0, L1_gnn_w2_vv1, L1_gnn_Ws_vlin, L1_gnn_Wv_vlin, L1_gnn_Wps, L1_gnn_Wpv, edge_index), axis=-1)
    return x

_drawn_inputs = setup_inputs


def setup_inputs(seed=0):
    import zlib

    import numpy as np

    out = dict(_drawn_inputs(seed))
    spreads = {'L1_gnn_gamma_s': (1.0, 0.2), 'L1_gnn_beta_s': (0.0, 0.311), 'L1_gnn_gamma_v': (1.0, 0.6)}
    factors = {'L0_gnn_Wfc1': 8.0,
     'L0_gnn_Wfc2': 8.0,
     'L0_gnn_Wl1_0': 8.0,
     'L0_gnn_Wl1_1': 8.0,
     'L0_gnn_Wl2_s': 8.0,
     'L0_gnn_Wl2_v': 8.0,
     'L0_gnn_Wa': 8.0,
     'L0_gnn_Wsc0': 8.0,
     'L0_gnn_Wsc1': 8.0}
    for name, (base, spread) in spreads.items():
        noise = np.random.default_rng([zlib.crc32(name.encode()), seed]).standard_normal(out[name].shape)
        drawn = base * np.exp(spread * noise) if base else spread * noise
        out[name] = jnp.asarray(drawn.astype(out[name].dtype))
    for name, factor in factors.items():
        out[name] = (out[name] * factor).astype(out[name].dtype)
    return out
```

```python
import concourse.bass as bass
from concourse import mybir
from contextlib import ExitStack
import numpy as np

P = 128
N, E = 12500, 200000
CS, CV = 64, 32
D = CS + 3 * CV
DX = CS + 5 * CV
FC, WN0, WN1 = 16, 192, 224
HEADS, AS, AV = 4, 16, 8
HW = AS + 3 * AV
K = 4
NP = 784
NT = 2 * NP
NI = NP // K
NPL = NP + K
NC = 13
NTC = NC * P
NB = 49
NN = NB * 2 * P
T0W = 4 * 96 + 2
T0I = T0W - 1
HR = HEADS * (HW + 1)
SKIP = 16384
BIG = 1.0e30
START = 16
META = 16
EPS = 1e-5

F32 = mybir.dt.float32
I32 = mybir.dt.int32
ALU = mybir.AluOpType
ACT = mybir.ActivationFunctionType
AX = mybir.AxisListType
W_COLS = {}


def wait_alone(eng, sem, value):
    if not isinstance(value, int):
        value = eng.snap(eng.to_reg(value))
    eng.wait_ge(sem, 0)
    eng.wait_ge(sem, value)


class Steps:

    def __init__(self, eng, sem):
        self.eng, self.sem, self.n, self.base = eng, sem, 0, 0

    def did(self, ins):
        ins.then_inc(self.sem, 1)
        self.n += 1
        return self.n

    def after(self, n):
        self.eng.wait_ge(self.sem, self.base + n)

    def after_alone(self, n):
        wait_alone(self.eng, self.sem, self.base + n)

    def link(self, ins):
        self.after(self.did(ins))


def build(nc, x, attr, meta, dstp, esT, wpack, wconst, out):
    top = ExitStack()
    dram = lambda name, shape, dt=F32: nc.dram_tensor(name, shape, dt).ap()
    F = dram("F_table", [NN, D])
    T0 = dram("T0_table", [NN, T0W])
    A = dram("A_table", [NN, DX])
    B = dram("B_table", [NN, DX])
    X1 = dram("X1_nodes", [NN, D])
    H = dram("H_messages", [NP, P, 2 * HR])
    T1 = dram("T1_table", [NN, HR])

    with top:
        sb = lambda name, shape, dt=F32: top.enter_context(nc.sbuf_tensor(name, shape, dt))
        wt = sb("wt", [P, wpack.shape[1]])
        wc = sb("wc", [P, wconst.shape[1]])
        ident = sb("ident", [P, P])
        iota = sb("iota", [P, P])
        tabs = sb("tabs", [P, 3, NTC])
        logit = sb("logit", [P, NTC, HEADS])
        rowidx = sb("rowidx", [P, NT], I32)
        attr_s = sb("attr_s", [P, 2 * NB])
        w1v = sb("w1v", [P, CV])
        w1c = sb("w1c", [P, 2, 320])
        w2 = sb("w2", [P, 5, D])
        gate_t = sb("gate_t", [P, 2, CV])
        seg_open = sb("seg_open", [P, NC, P])
        seg_shut = sb("seg_shut", [P, NC, P])
        not_first = sb("not_first", [P, NC, P])
        not_last = sb("not_last", [P, NC, P])
        one_seg = sb("one_seg", [P, NC, HEADS])
        goes_on = sb("goes_on", [P, NC, HEADS])
        W = lambda name: wt[:W_COLS[name][1], W_COLS[name][0]:W_COLS[name][0] + W_COLS[name][2]]
        C = lambda j: wc[:, j:j + 1]

        prep(nc, locals())
        nodes0(nc, locals())
        edges0(nc, locals())
        nodes1(nc, locals())
        edges1(nc, locals())
        softmax(nc, locals())
        edges2(nc, locals())
        nodes2(nc, locals())


class Stage:

    def __init__(self, nc, name):
        self.nc, self.name, self.stack = nc, name, ExitStack()

    def __enter__(self):
        return self

    def __exit__(self, *a):
        self.stack.close()

    def sb(self, name, shape, dt=F32):
        return self.stack.enter_context(self.nc.sbuf_tensor(f"{self.name}_{name}", shape, dt))

    def ps(self, name, shape, dt=F32):
        return self.stack.enter_context(self.nc.psum_tensor(f"{self.name}_{name}", shape, dt))

    def sem(self, name):
        return self.stack.enter_context(self.nc.semaphore(f"{self.name}_{name}"))


def prep(nc, v):
    wt, wc, ident, iota, tabs, logit = v["wt"], v["wc"], v["ident"], v["iota"], v["tabs"], v["logit"]
    W, C = v["W"], v["C"]
    w1v, w1c, w2, gate_t = v["w1v"], v["w1c"], v["w2"], v["gate_t"]
    dstp = v["dstp"]
    with Stage(nc, "prep") as st:
        shifts = [0, -1, 1, -P, -P - 1]
        four = logit[:, :, :].bitcast(I32).rearrange("p t h -> p (t h)").rearrange("p (k c e) -> p k c e", k=4, e=P)
        fifth = st.sb("fifth", [P, NC, P], I32)
        ints = [four[:, k] for k in range(4)] + [fifth[:, :, :]]
        dst = st.sb("dst", [P, 5, NC, P])
        opens, opens_before, ends = v["seg_open"], v["not_first"], v["seg_shut"]
        last_rank = st.sb("last_rank", [P, NC])
        byt = st.sb("byt", [P, 3, NC, P])
        zero = st.sb("zero", [P, 512])
        cont = st.sb("cont", [P, NC])
        single = st.sb("single", [P, NC])
        tp = st.ps("tp", [P, 2, 512])
        gp = st.ps("gp", [P, 2, 512])
        loaded, made, built = st.sem("loaded"), st.sem("made"), st.sem("built")
        turned, kept, cleared, step = st.sem("turned"), st.sem("kept"), st.sem("cleared"), st.sem("step")
        gates, zeroed = st.sem("gates"), st.sem("zeroed")
        T0, T1 = v["T0"], v["T1"]
        jobs = [(k, c) for k in range(3) for c in range(NC)]
        batches = [jobs[a:a + 4] for a in range(0, len(jobs), 4)]
        with nc.Block() as block:

            @block.sync
            def _(sp):
                sp.dma_start(wt[:, :], v["wpack"]).then_inc(loaded, 16)
                sp.dma_start(wc[:, :], v["wconst"]).then_inc(loaded, 16)
                sp.dma_start(v["attr_s"][:, :], v["attr"]).then_inc(loaded, 16)
                for k, s in enumerate(shifts):
                    src = dstp[P + 1 + s:P + 1 + s + NTC * P].rearrange("(c p e) -> p c e", p=P, e=P)
                    sp.dma_start(ints[k], src).then_inc(loaded, 16)
                sp.wait_ge(zeroed, 1)
                n = 0
                for table, width in ((T0, T0W), (T1, HR)):
                    flat = table.rearrange("n w -> (n w)").rearrange("(q p w) -> q p w", p=P, w=width)
                    for q in range(2 * NB):
                        sp.dma_start(flat[q], zero[:, :width]).then_inc(cleared, 16)
                        n += 16
                sp.wait_ge(cleared, n)

            @block.gpsimd
            def _(pool):
                nc.gpsimd.memset(ident[:, :], 0.0).then_inc(made, 1)
                nc.gpsimd.iota(iota[:, :], [[1, P]], base=0, channel_multiplier=0,
                               allow_small_or_imprecise_dtypes=True).then_inc(made, 1)
                pool.wait_ge(made, 2)
                nc.gpsimd.affine_select(out=ident[:, :], in_=ident[:, :], compare_op=ALU.not_equal, fill=1.0,
                                        base=0, pattern=[[-1, P]], channel_multiplier=1).then_inc(made, 1)

            @block.vector
            def _(dve):
                V = nc.vector
                s = Steps(dve, step)
                V.memset(zero[:, :], 0.0).then_inc(zeroed, 1)
                dve.wait_ge(loaded, 16 * 8)
                dve.wait_ge(made, 3)
                for name, const in (("fc1", 1 / 4), ("fc2", 1 / 8), ("l1_0", 1 / 8), ("sc0", 1 / 8),
                                    ("l1_1", CV ** -0.5), ("sc1", CV ** -0.5), ("l2v", 96 ** -0.5)):
                    s.link(V.tensor_scalar(W(name), W(name), const, None, ALU.mult))
                s.link(V.tensor_scalar(W("l2s"), W("l2s"), wc[:96, 0:1], None, ALU.mult))
                s.link(V.tensor_scalar(w1v[:, :], W("wv_val"), C(1), None, ALU.mult))
                for c in range(2):
                    s.link(V.tensor_scalar(w1c[:, c, :], W(f"w1c{c}"), C(2 + c), None, ALU.mult))
                for c in range(5):
                    s.link(V.tensor_scalar(w2[:, c, :], W(f"w2_{c}"), C(4 + c), wt[:, W_COLS["w2s"][0] + c:W_COLS["w2s"][0] + c + 1],
                                           ALU.mult, ALU.mult))
                dve.wait_ge(gates, 2)
                for c in range(2):
                    s.link(V.tensor_scalar(w1c[:, c, 128:160], gp[:, c, :CV], C(2 + c), None, ALU.mult))
                for k in range(5):
                    s.did(V.tensor_copy(dst[:, k], ints[k]))
                s.after(s.n)
                s.did(V.memset(logit[:, NT:, :], 0.0))
                this, before, behind, tile_before, before_that = (dst[:, k] for k in range(5))
                s.did(V.tensor_tensor(opens[:, :, :], this, before, ALU.not_equal))
                s.did(V.tensor_tensor(opens_before[:, :, :], tile_before, before_that, ALU.not_equal))
                s.did(V.tensor_tensor(ends[:, :, :], this, behind, ALU.not_equal))
                s.link(V.tensor_tensor(cont[:, :], this[:, :, 0], before[:, :, 0], ALU.is_equal))
                s.did(V.memset(opens[:, :, 0:1], 0.0))
                s.link(V.memset(opens_before[:, :, 0:1], 0.0))
                for c in range(NC):
                    s.did(V.tensor_tensor_scan(byt[:, 0, c], opens[:, c], zero[:, :P], 0.0, ALU.add, ALU.add))
                    s.did(V.tensor_tensor_scan(byt[:, 2, c], opens_before[:, c], zero[:, :P], 0.0, ALU.add, ALU.add))
                s.link(V.scalar_tensor_tensor(byt[:, 1], this, float(-SKIP), ends[:, :, :], ALU.add, ALU.mult))
                s.link(V.tensor_copy(last_rank[:, :], byt[:, 2, :, P - 1]))
                for c in range(NC):
                    s.did(V.tensor_scalar(byt[:, 2, c], iota[:, :], last_rank[:, c:c + 1], cont[:, c:c + 1],
                                          ALU.is_equal, ALU.mult))
                rank = byt[:, 0]
                s.did(V.tensor_scalar(opens[:, :, :], opens[:, :, :], -BIG, None, ALU.mult))
                s.did(V.tensor_scalar(ends[:, :, :], ends[:, :, :], -BIG, None, ALU.mult))
                s.did(V.tensor_scalar(v["not_first"][:, :, :], rank, 0.0, -BIG, ALU.not_equal, ALU.mult))
                for c in range(NC):
                    s.did(V.tensor_scalar(v["not_last"][:, c], rank[:, c], rank[:, c, P - 1:P], -BIG, ALU.not_equal, ALU.mult))
                s.link(V.tensor_scalar(single[:, :], rank[:, :, P - 1], 0.0, None, ALU.is_equal))
                s.did(V.memset(v["seg_open"][:, :, 0:1], -BIG))
                s.did(V.memset(v["seg_shut"][:, :, P - 1:P], -BIG))
                s.did(V.tensor_copy(v["one_seg"][:, :, :], single[:, :].unsqueeze(2).broadcast_to([P, NC, HEADS])))
                V.tensor_copy(v["goes_on"][:, :, :], cont[:, :].unsqueeze(2).broadcast_to([P, NC, HEADS])).then_inc(built, 1)

            @block.tensor
            def _(pe):
                pe.wait_ge(loaded, 16 * 8)
                for c in range(2):
                    nc.tensor.matmul(gp[:, c, :CV], W(f"ws_valT{c}"), W("wg"), start=True, stop=True).then_inc(gates, 1)
                pe.wait_ge(made, 3)
                pe.wait_ge(built, 1)
                for b, batch in enumerate(batches):
                    if b >= 2:
                        pe.wait_ge(kept, b - 1)
                    for q, (k, c) in enumerate(batch):
                        last = nc.tensor.transpose(tp[:, b % 2, q * P:(q + 1) * P], byt[:, k, c], ident[:, :])
                    last.then_inc(turned, 1)

            @block.scalar
            def _(act):
                flat = tabs[:, :, :].rearrange("p k t -> p (k t)")
                for b, batch in enumerate(batches):
                    act.wait_ge(turned, b + 1)
                    w = len(batch) * P
                    nc.scalar.activation(flat[:, b * 512:b * 512 + w], tp[:, b % 2, :w], ACT.Copy).then_inc(kept, 1)
                act.wait_ge(kept, len(batches))


def nodes0(nc, v):
    W, ident = v["W"], v["ident"]
    x3 = v["x"].rearrange("(b j p) w -> b p j w", j=2, p=P)
    f3 = v["F"].rearrange("(b j p) w -> b p j w", j=2, p=P)
    with Stage(nc, "nodes0") as st:
        xs = st.sb("xs", [P, 2, D])
        xT = st.sb("xT", [P, 2, 256])
        fs = st.sb("fs", [P, 2, D])
        tp, fp = st.ps("tp", [P, 2, 256]), st.ps("fp", [P, 2, D])
        loaded, turned, kept = st.sem("loaded"), st.sem("turned"), st.sem("kept")
        product, scaled, stored = st.sem("product"), st.sem("scaled"), st.sem("stored")
        with nc.Block() as block:

            @block.sync
            def _(sp):
                with sp.Fori(0, NB) as b:
                    sp.wait_ge(turned, b)
                    sp.dma_start(xs[:, :, :], x3[bass.ds(b, 1)].rearrange("o p j w -> (o p) j w")).then_inc(loaded, 16)
                    sp.wait_ge(scaled, 2 * b + 2)
                    sp.dma_start(f3[bass.ds(b, 1)].rearrange("o p j w -> (o p) j w"), fs[:, :, :]).then_inc(stored, 16)
                sp.wait_ge(stored, 16 * NB)

            @block.tensor
            def _(pe):
                with pe.Fori(0, NB) as b:
                    pe.wait_ge(loaded, 16 * b + 16)
                    wait_alone(pe, kept, 2 * b)
                    for j in range(2):
                        nc.tensor.transpose(tp[:CS, j, :P], xs[:, j, :CS], ident[:, :])
                        last = nc.tensor.transpose(tp[:96, j, P:], xs[:, j, CS:], ident[:, :])
                    last.then_inc(turned, 1)
                    pe.wait_ge(kept, 2 * b + 2)
                    pe.wait_ge(scaled, 2 * b)
                    for j in range(2):
                        nc.tensor.matmul(fp[:, j, :CS], xT[:CS, j, :P], W("l1_0"), start=True, stop=True)
                        last = nc.tensor.matmul(fp[:, j, CS:], xT[:96, j, P:], W("l1_1"), start=True, stop=True)
                    last.then_inc(product, 1)

            @block.scalar
            def _(act):
                with act.Fori(0, NB) as b:
                    act.wait_ge(turned, b + 1)
                    act.wait_ge(product, b)
                    nc.scalar.activation(xT[:CS, :, :P], tp[:CS, :, :P], ACT.Copy).then_inc(kept, 1)
                    nc.scalar.activation(xT[:96, :, P:], tp[:96, :, P:], ACT.Copy).then_inc(kept, 1)
                    act.wait_ge(product, b + 1)
                    act.wait_ge(stored, 16 * b)
                    for j in range(2):
                        nc.scalar.activation(fs[:, j, :], fp[:, j, :], ACT.Copy,
                                             scale=v["attr_s"][:, bass.ds(2 * b + j, 1)]).then_inc(scaled, 1)


def edges0(nc, v):
    W, iota, tabs = v["W"], v["iota"], v["tabs"]
    with Stage(nc, "edges0") as st:
        rec = st.sb("rec", [P, K, META], I32)
        es = st.sb("es", [FC, K, 256])
        feat = st.sb("feat", [P, K, 2, D])
        hT = st.sb("hT", [CS, 2, 256])
        e1y = st.sb("e1y", [P, 2, 2, 96])
        dot = st.sb("dot", [P, 2, 2, CV])
        p01 = st.sb("p01", [P, 2, 2, 2, CS])
        w2y = st.sb("w2y", [P, 2, 2, CV])
        mid = st.sb("mid", [P, 2, 2, T0W])
        onehot = st.sb("onehot", [P, 2, 2, P])
        carry = st.sb("carry", [P, 2, 2])
        acc = st.sb("acc", [P, K, T0W])
        rows = st.sb("rows", [P, K], I32)
        hp, wp = st.ps("hp", [CS, 2, 512]), st.ps("wp", [P, 2, 512])
        sp_ = st.ps("sums", [P, 2, 512])
        loaded = [st.sem(f"loaded{k}") for k in range(K)]
        gathered = [st.sem(f"gathered{k}") for k in range(K)]
        scattered = [st.sem(f"scattered{k}") for k in range(K)]
        h_done, silu_done, w_done = st.sem("h_done"), st.sem("silu_done"), st.sem("w_done")
        mid_done, sum_done, kept, step = st.sem("mid_done"), st.sem("sum_done"), st.sem("kept"), st.sem("step")
        ones = st.sem("ones")
        y = [rec[:, k, 4:].bitcast(F32).rearrange("p (j c) -> p j c", j=2) for k in range(K)]
        with nc.Block() as block:

            @block.sync
            def _(sp):
                with sp.Fori(0, NPL // K) as i:
                    for k in range(K):
                        load_pair(sp, v, rec, es, loaded, gathered, h_done, mid_done, i, k)
                for k in range(K):
                    sp.wait_ge(loaded[k], 32 * (NPL // K))
                    sp.wait_ge(gathered[k], 32 * (NI + (k < 3)))

            @block.gpsimd
            def _(pool):
                def gather(i, k):
                    slot, use = k % K, i + k // K
                    wait_alone(pool, loaded[slot], 32 * use + 32)
                    wait_alone(pool, mid_done, START + K * i + k - K + 1)
                    for j in range(2):
                        nc.gpsimd.indirect_dma_start(feat[:, slot, j, :], None, v["F"], bass.IndirectOffsetOnAxis(
                            ap=rec[:, slot, j:j + 1], axis=0)).then_inc(gathered[slot], 16)

                for k in range(3):
                    gather(0, k)
                with pool.Fori(0, NI) as i:
                    for k in range(K):
                        gather(i, k + 3)
                        scatter(nc, pool, v["T0"], acc, rows, T0W, kept, scattered, i, k)
                scatter_end(pool, scattered)

            @block.scalar
            def _(act):
                act.sem_inc(silu_done, START)
                act.sem_inc(kept, START)

                def silu(i, k):
                    act.wait_ge(h_done, START + K * i + k + 1)
                    act.wait_ge(w_done, START + K * i + k - 1)
                    nc.scalar.activation(hT[:, k % 2, :], hp[:, k % 2, :256], ACT.Silu).then_inc(silu_done, 1)

                for k in range(2):
                    silu(0, k)
                with act.Fori(0, NI) as i:
                    for k in range(K):
                        silu(i, k + 2)
                        keep_sums(nc, act, sp_, acc, rows, T0W, v["rowidx"], sum_done, kept, scattered, i, k)

            @block.tensor
            def _(pe):
                pe.sem_inc(h_done, START)
                pe.sem_inc(w_done, START)
                pe.sem_inc(sum_done, START)

                def hidden(i, k):
                    slot = k % K
                    pe.wait_ge(loaded[slot], 32 * (i + k // K) + 32)
                    pe.wait_ge(silu_done, START + K * i + k - 1)
                    nc.tensor.matmul(hp[:, k % 2, :256], W("fc1"), es[:, slot, :], start=True, stop=True).then_inc(h_done, 1)

                def weights(i, k):
                    pe.wait_ge(silu_done, START + K * i + k + 1)
                    pe.wait_ge(mid_done, START + K * i + k - 1)
                    for j in range(2):
                        last = nc.tensor.matmul(wp[:, k % 2, j * WN0:(j + 1) * WN0], hT[:, k % 2, j * P:(j + 1) * P],
                                                W("fc2"), start=True, stop=True)
                    last.then_inc(w_done, 1)

                hidden(0, 0)
                hidden(0, 1)
                weights(0, 0)
                pe.wait_ge(ones, 1)
                with pe.Fori(0, NI) as i:
                    for k in range(K):
                        hidden(i, k + 2)
                        weights(i, k + 1)
                        pe.wait_ge(mid_done, START + K * i + k + 1)
                        sum_segments(nc, pe, onehot, mid, carry, acc, sp_, T0W, kept, sum_done, i, k)

            @block.vector
            def _(dve):
                V = nc.vector
                dve.sem_inc(mid_done, START)
                s = Steps(dve, step)
                for q in range(2):
                    s.did(V.memset(mid[:, q, :, T0W - 2:T0W - 1], 1.0))
                s.link(V.memset(acc[:, :, :], 0.0))
                dve.sem_inc(ones, 1)
                PER = 12
                first = s.n
                with dve.Fori(0, NI) as i:
                    s.n = 0
                    s.base = first + K * PER * i
                    for k in range(K):
                        slot, q = k, k % 2
                        e0, e1 = feat[:, slot, :, :CS], feat[:, slot, :, CS:].rearrange("p j (m u) -> p j m u", m=3)
                        w = wp[:, q, :2 * WN0].rearrange("p (j w) -> p j w", j=2)
                        ys = y[slot]
                        one = lambda c, n: ys[:, :, c:c + 1].broadcast_to([P, 2, n])
                        three = lambda n: ys[:, :, 1:4].unsqueeze(3).broadcast_to([P, 2, 3, n])
                        row = mid[:, q]
                        scal1 = row[:, :, CS:96]
                        vec = row[:, :, 96:384].rearrange("p j (m w) -> p j m w", m=3)
                        dve.wait_ge(gathered[slot], 32 * i + 32)
                        dve.wait_ge(sum_done, START + 2 * (K * i + k - 2) + 2)
                        a = s.did(V.tensor_tensor(e1y[:, q].rearrange("p j (m u) -> p j m u", m=3), e1, three(CV), ALU.mult))
                        s.did(V.tensor_tensor(onehot[:, q], tabs[:, 0, bass.ds(2 * (K * i + k), 2)].unsqueeze(2).broadcast_to([P, 2, P]),
                                              iota[:, :].unsqueeze(1).broadcast_to([P, 2, P]), ALU.is_equal))
                        s.after(a)
                        b = s.did(V.tensor_tensor(dot[:, q], e1y[:, q, :, :CV], e1y[:, q, :, CV:2 * CV], ALU.add))
                        dve.wait_ge(w_done, START + K * i + k + 1)
                        c = s.did(V.tensor_tensor(p01[:, q], w[:, :, :2 * CS].rearrange("p j (a u) -> p j a u", a=2),
                                                  e0.unsqueeze(2).broadcast_to([P, 2, 2, CS]), ALU.mult))
                        s.after(b)
                        b = s.did(V.tensor_tensor(dot[:, q], dot[:, q], e1y[:, q, :, 2 * CV:], ALU.add))
                        d = s.did(V.tensor_tensor(w2y[:, q], w[:, :, 128:160], one(0, CV), ALU.mult))
                        s.after(c)
                        s.did(V.tensor_tensor(vec[:, :, :, :CS], p01[:, q, :, 1].unsqueeze(2).broadcast_to([P, 2, 3, CS]),
                                              three(CS), ALU.mult))
                        s.did(V.tensor_tensor(row[:, :, :CS], p01[:, q, :, 0], one(0, CS), ALU.mult))
                        s.after(d)
                        s.did(V.tensor_tensor(vec[:, :, :, CS:], e1, w2y[:, q].unsqueeze(2).broadcast_to([P, 2, 3, CV]), ALU.mult))
                        s.did(V.tensor_tensor(scal1, w[:, :, 160:192], dot[:, q], ALU.mult))
                        s.did(V.tensor_copy(row[:, :, T0I], tabs[:, 1, bass.ds(2 * (K * i + k), 2)]))
                        s.did(V.tensor_copy(carry[:, q], tabs[:, 2, bass.ds(2 * (K * i + k), 2)]))
                        s.after(s.n)
                        V.memset(row[:, :, T0W - 2:T0W - 1], 1.0).then_inc(mid_done, 1)
                    assert s.n == K * PER, s.n


def load_pair(sp, v, rec, es, loaded, ids_read, es_read, y_read, i, k):
    slot, use = k % K, i + k // K
    wait_alone(sp, ids_read[slot], 32 * use)
    wait_alone(sp, es_read, START + K * i + k - K + 1)
    wait_alone(sp, y_read, START + K * i + k - K + 1)
    sp.dma_start(rec[:, slot, :], v["meta"][bass.ds(K * i + k, 1)].rearrange("o p w -> (o p) w")).then_inc(loaded[slot], 16)
    sp.dma_start(es[:, slot, :], v["esT"][:, bass.ds(256 * (K * i + k), 256)]).then_inc(loaded[slot], 16)


def sum_segments(nc, pe, onehot, vals, carry, acc, sums, width, kept, sum_done, i, k):
    q = k % 2
    for j in range(2):
        slot = 2 * q + j
        pe.wait_ge(kept, START + 2 * (K * i + k) + j - 1)
        nc.tensor.matmul(sums[:, j, :width], onehot[:, q, j, :], vals[:, q, j, :], start=True, stop=True)
        pe.wait_ge(kept, START + 2 * (K * i + k) + j)
        nc.tensor.matmul(sums[:1, j, :width], carry[:, q, j:j + 1], acc[:, (slot - 1) % K, :width],
                         start=False, stop=True, skip_group_check=True).then_inc(sum_done, 1)


def keep_sums(nc, act, sums, acc, rows, width, rowidx, sum_done, kept, scattered, i, k):
    for j in range(2):
        slot = 2 * (k % 2) + j
        act.wait_ge(sum_done, START + 2 * (K * i + k) + j + 1)
        act.wait_ge(scattered[slot], 16 * (2 * i + k // 2))
        nc.scalar.activation(rowidx[:, bass.ds(2 * (K * i + k) + j, 1)], sums[:, j, width - 1:width], ACT.Copy, bias=float(SKIP))
        nc.scalar.activation(rows[:, slot:slot + 1], sums[:, j, width - 1:width], ACT.Copy, bias=float(SKIP))
        nc.scalar.activation(acc[:, slot, :width], sums[:, j, :width], ACT.Copy).then_inc(kept, 1)


def scatter(nc, pool, table, acc, rows, width, kept, scattered, i, k):
    for j in range(2):
        slot = 2 * (k % 2) + j
        wait_alone(pool, kept, START + 2 * (K * i + k) + j + 1)
        nc.gpsimd.indirect_dma_start(table, bass.IndirectOffsetOnAxis(ap=rows[:, slot:slot + 1], axis=0),
                                     acc[:, slot, :width], None, bounds_check=N - 1, oob_is_err=False).then_inc(scattered[slot], 16)


def scatter_end(pool, scattered):
    for s in scattered:
        pool.wait_ge(s, 16 * (NT // K))


def layer_norm(V, s, act_root, stats, mv, var, rstd, row, j2, width=D):
    for j in range(j2):
        s.did(V.bn_stats(stats[:, j, :], row[:, j, :width]))
    s.after_alone(s.n)
    for j in range(j2):
        s.did(V.bn_aggr(mv[:, j, :], stats[:, j, :]))
    s.after(s.n)
    act_root(V.tensor_scalar(var[:, :], mv[:, :, 1], EPS, None, ALU.add))


def nodes1(nc, v):
    W, ident = v["W"], v["ident"]
    rows_of = lambda t: t.rearrange("(b j p) w -> b p j w", j=2, p=P)
    x3, t3, x13, a3, b3 = (rows_of(v[k]) for k in ("x", "T0", "X1", "A", "B"))
    at = lambda t, b: t[bass.ds(b, 1)].rearrange("o p j w -> (o p) j w")
    with Stage(nc, "nodes1") as st:
        xs, ts = st.sb("xs", [P, 2, D]), st.sb("ts", [P, 2, T0W])
        xT, tT = st.sb("xT", [P, 2, 256]), st.sb("tT", [P, 2, 512])
        nT = st.sb("nT", [P, 2, 256])
        per = st.sb("per", [P, 4, 2])
        ya, yb, x1 = st.sb("ya", [P, 2, D]), st.sb("yb", [P, 2, D]), st.sb("x1", [P, 2, D])
        sq, norm, norm2 = st.sb("sq", [P, 2, 96]), st.sb("norm", [P, 2, D]), st.sb("norm2", [P, 2, D])
        stats, mv = st.sb("stats", [P, 2, 6]), st.sb("mv", [P, 2, 2])
        var, root, rstd = (st.sb(n, [P, 2]) for n in ("var", "root", "rstd"))
        var2, root2, rstd2 = (st.sb(n, [P, 2, 2]) for n in ("var2", "root2", "rstd2"))
        ab = st.sb("ab", [P, 2, 2 * DX])
        tp, cp = st.ps("tp", [P, 2, 512]), st.ps("cp", [P, 2, 512])
        xp, abp = st.ps("xp", [P, 2, 256]), st.ps("abp", [P, 2, 512])
        sem = {n: st.sem(n) for n in ("loaded", "turned", "kept", "conv", "varied", "rooted", "x1_done", "norm_done",
                                      "turned2", "kept2", "ab_done", "ab_kept", "stored", "step")}
        with nc.Block() as block:

            @block.sync
            def _(sp):
                with sp.Fori(0, NB) as b:
                    sp.wait_ge(sem["x1_done"], b)
                    sp.dma_start(ts[:, :, :], at(t3, b)).then_inc(sem["loaded"], 16)
                    sp.dma_start(xs[:, :, :], at(x3, b)).then_inc(sem["loaded"], 16)
                    sp.wait_ge(sem["x1_done"], b + 1)
                    sp.dma_start(at(x13, b), x1[:, :, :]).then_inc(sem["stored"], 16)
                    sp.wait_ge(sem["ab_kept"], b + 1)
                    sp.dma_start(at(a3, b), ab[:, :, :DX]).then_inc(sem["stored"], 16)
                    sp.dma_start(at(b3, b), ab[:, :, DX:]).then_inc(sem["stored"], 16)
                sp.wait_ge(sem["stored"], 48 * NB)

            @block.tensor
            def _(pe):
                T = nc.tensor
                with pe.Fori(0, NB) as b:
                    pe.wait_ge(sem["loaded"], 32 * b + 32)
                    for j in range(2):
                        for c in range(4):
                            T.transpose(tp[:96, j, c * P:(c + 1) * P], ts[:, j, 96 * c:96 * c + 96], ident[:, :])
                        T.transpose(xp[:CS, j, :P], xs[:, j, :CS], ident[:, :])
                        last = T.transpose(xp[:96, j, P:], xs[:, j, CS:], ident[:, :])
                    last.then_inc(sem["turned"], 1)
                    pe.wait_ge(sem["kept"], b + 1)
                    for j in range(2):
                        T.matmul(cp[:, j, :CS], tT[:96, j, :P], W("l2s")[:, :CS], start=True, stop=True)
                        T.matmul(cp[:, j, D:D + 1], tT[:96, j, :P], W("l2s")[:, CS:CS + 1], start=True, stop=True)
                        for m in range(3):
                            T.matmul(cp[:, j, CS + m:D:3], tT[:96, j, (m + 1) * P:(m + 2) * P], W("l2v"), start=True, stop=True)
                        T.matmul(cp[:, j, 164:164 + CS], xT[:CS, j, :P], W("sc0"), start=True, stop=True)
                        last = T.matmul(cp[:, j, 164 + CS:164 + D], xT[:96, j, P:], W("sc1"), start=True, stop=True)
                    last.then_inc(sem["conv"], 1)
                    wait_alone(pe, sem["norm_done"], b + 1)
                    for j in range(2):
                        T.transpose(xp[:CS, j, :P], norm[:, j, :CS], ident[:, :])
                        last = T.transpose(xp[:96, j, P:], norm2[:, j, CS:], ident[:, :])
                    last.then_inc(sem["turned2"], 1)
                    pe.wait_ge(sem["kept2"], b + 1)
                    for j in range(2):
                        for o, s_, v_ in ((0, "ws_src", "wv_src"), (DX, "ws_dst", "wv_dst")):
                            T.matmul(abp[:, j, o:o + CS], nT[:CS, j, :P], W(s_), start=True, stop=True)
                            last = T.matmul(abp[:, j, o + CS:o + DX], nT[:96, j, P:], W(v_), start=True, stop=True)
                    last.then_inc(sem["ab_done"], 1)

            @block.scalar
            def _(act):
                S = nc.scalar
                with act.Fori(0, NB) as b:
                    act.wait_ge(sem["turned"], b + 1)
                    S.activation(tT[:96, :, :], tp[:96, :, :], ACT.Copy)
                    S.activation(xT[:CS, :, :P], xp[:CS, :, :P], ACT.Copy)
                    S.activation(xT[:96, :, P:], xp[:96, :, P:], ACT.Copy).then_inc(sem["kept"], 1)
                    act.wait_ge(sem["varied"], 2 * b + 1)
                    S.activation(root[:, :], var[:, :], ACT.Sqrt).then_inc(sem["rooted"], 1)
                    act.wait_ge(sem["varied"], 2 * b + 2)
                    S.activation(root2[:, :, :], var2[:, :, :], ACT.Sqrt).then_inc(sem["rooted"], 1)
                    act.wait_ge(sem["turned2"], b + 1)
                    S.activation(nT[:CS, :, :P], xp[:CS, :, :P], ACT.Copy)
                    S.activation(nT[:96, :, P:], xp[:96, :, P:], ACT.Copy).then_inc(sem["kept2"], 1)
                    act.wait_ge(sem["ab_done"], b + 1)
                    act.wait_ge(sem["stored"], 48 * b)
                    S.activation(ab[:, :, :], abp[:, :, :2 * DX], ACT.Copy).then_inc(sem["ab_kept"], 1)

            @block.vector
            def _(dve):
                V = nc.vector
                s = Steps(dve, sem["step"])
                PER = 29
                with dve.Fori(0, NB) as b:
                    s.n, s.base = 0, PER * b

                    def rooted(ins, n):
                        ins.then_inc(sem["varied"], 1)
                        dve.wait_ge(sem["rooted"], 2 * b + n)

                    al, r, cnt, rc = (per[:, q, :] for q in range(4))
                    dve.wait_ge(sem["loaded"], 32 * b + 32)
                    s.link(V.tensor_scalar(cnt, ts[:, :, T0W - 2], 1.0, None, ALU.max))
                    s.link(V.reciprocal(rc, cnt))
                    s.link(V.tensor_tensor(r, rc, v["attr_s"][:, bass.ds(2 * b, 2)], ALU.mult))
                    s.link(V.tensor_tensor(cnt, r, r, ALU.mult))
                    dve.wait_ge(sem["conv"], b + 1)
                    s.did(V.tensor_tensor(al, cnt, cp[:, :, D], ALU.mult))
                    for j in range(2):
                        s.did(V.scalar_tensor_tensor(ya[:, j, :], cp[:, j, 164:164 + D], v["attr_s"][:, bass.ds(2 * b + j, 1)],
                                                     xs[:, j, :], ALU.mult, ALU.add))
                    s.after(s.n)
                    for j in range(2):
                        s.did(V.scalar_tensor_tensor(yb[:, j, :], cp[:, j, :D], al[:, j:j + 1], ya[:, j, :], ALU.mult, ALU.add))
                    s.after(s.n)
                    layer_norm(V, s, lambda ins: rooted(ins, 1), stats, mv, var, rstd, yb, 2)
                    s.link(V.reciprocal(rstd[:, :], root[:, :]))
                    dve.wait_ge(sem["stored"], 48 * b)
                    for j in range(2):
                        s.did(V.tensor_scalar(x1[:, j, :], yb[:, j, :], mv[:, j, 0:1], rstd[:, j:j + 1], ALU.subtract, ALU.mult))
                    s.after(s.n)
                    V.tensor_tensor(sq[:, :, :], x1[:, :, CS:], x1[:, :, CS:], ALU.mult).then_inc(sem["x1_done"], 1)
                    for j in range(2):
                        s.did(V.bn_stats(stats[:, j, :], x1[:, j, :CS]))
                    s.after_alone(s.n)
                    for j in range(2):
                        s.did(V.bn_aggr(mv[:, j, :], stats[:, j, :]))
                    dve.wait_ge(sem["x1_done"], b + 1)
                    s.link(V.tensor_reduce(per[:, 3, :], sq[:, :, :], AX.X, ALU.add))
                    s.did(V.tensor_scalar(var2[:, 1, :], per[:, 3, :], 1.0 / CV, EPS, ALU.mult, ALU.add))
                    rooted(V.tensor_scalar(var2[:, 0, :], mv[:, :, 1], EPS, None, ALU.add), 2)
                    s.link(V.reciprocal(rstd2[:, :, :], root2[:, :, :]))
                    dve.wait_ge(sem["turned2"], b)
                    for j in range(2):
                        s.did(V.tensor_scalar(norm[:, j, :CS], x1[:, j, :CS], mv[:, j, 0:1], rstd2[:, 0, j:j + 1], ALU.subtract, ALU.mult))
                        s.did(V.tensor_scalar(norm[:, j, CS:], x1[:, j, CS:], rstd2[:, 1, j:j + 1], None, ALU.mult))
                    s.after(s.n)
                    s.did(V.tensor_tensor(norm2[:, :, :CS], norm[:, :, :CS], W("gamma_s").unsqueeze(1).broadcast_to([P, 2, CS]), ALU.mult))
                    s.did(V.tensor_tensor(norm2[:, :, CS:].rearrange("p j (u m) -> p j u m", m=3),
                                          norm[:, :, CS:].rearrange("p j (u m) -> p j u m", m=3),
                                          W("gamma_v").unsqueeze(1).unsqueeze(3).broadcast_to([P, 2, CV, 3]), ALU.mult))
                    s.after(s.n)
                    V.tensor_tensor(norm[:, :, :CS], norm2[:, :, :CS], W("beta_s").unsqueeze(1).broadcast_to([P, 2, CS]),
                                    ALU.add).then_inc(sem["norm_done"], 1)
                    assert s.n == PER, s.n


def edges1(nc, v):
    W = v["W"]
    with Stage(nc, "edges1") as st:
        rec = st.sb("rec", [P, K, META], I32)
        es = st.sb("es", [FC, K, 256])
        msg = st.sb("msg", [P, K, 2, DX])
        yk = st.sb("yk", [P, K, 2, 6])
        pw = st.sb("pw", [P, 2, 2, 2, CS])
        wy = st.sb("wy", [P, 2, 2, CV])
        qv = st.sb("qv", [P, 2, 2, 96])
        qc = st.sb("qc", [P, 2, 2, 5 * CV])
        prod1, prod2 = st.sb("prod1", [P, 2, 2, 640]), st.sb("prod2", [P, 2, 2, 640])
        pt1, pt2 = st.sb("pt1", [P, 2, 640]), st.sb("pt2", [P, 2, 640])
        a_sb = st.sb("a_sb", [P, 2, 2, CS])
        sig = st.sb("sig", [P, 2, 2, 96])
        lr, la = st.sb("lr", [P, 2, 2, CS]), st.sb("la", [P, 2, 2, CS])
        vg = st.sb("vg", [P, 2, 2, 5 * CV])
        hs = st.sb("hs", [P, K, 2, HEADS, HW + 1])
        wp, xp, yp = st.ps("wp", [P, 2, 512]), st.ps("xp", [P, 2, 512]), st.ps("yp", [P, 2, P])
        op, hp = st.ps("op", [P, 2, 512]), st.ps("hp", [P, 2, 256])
        loaded = [st.sem(f"loaded{k}") for k in range(K)]
        from_src = [st.sem(f"from_src{k}") for k in range(K)]
        from_dst = [st.sem(f"from_dst{k}") for k in range(K)]
        stored = [st.sem(f"stored{k}") for k in range(K)]
        w_done, prod1_done, prod2_done = st.sem("w_done"), st.sem("prod1_done"), st.sem("prod2_done")
        turned, kept, s1_done, sig_done = st.sem("turned"), st.sem("kept"), st.sem("s1_done"), st.sem("sig_done")
        op_read, h_done, h_kept, step = st.sem("op_read"), st.sem("h_done"), st.sem("h_kept"), st.sem("step")
        ones = st.sem("ones")
        with nc.Block() as block:

            @block.sync
            def _(sp):
                load = lambda i, k: load_pair(sp, v, rec, es, loaded, from_dst, w_done, prod1_done, i, k)
                for k in range(K):
                    load(0, k)
                with sp.Fori(0, NI) as i:
                    for k in range(K):
                        load(i, k + K)
                        sp.wait_ge(h_kept, START + K * i + k + 1)
                        sp.dma_start(v["H"][bass.ds(K * i + k, 1)].rearrange("o p w -> (o p) w"),
                                     hs[:, k].rearrange("p j h w -> p (j h w)")).then_inc(stored[k], 16)
                for k in range(K):
                    sp.wait_ge(stored[k], 16 * NI)
                    sp.wait_ge(loaded[k], 32 * (NPL // K))

            @block.gpsimd
            def _(pool):
                def source(i, k):
                    slot, use = k % K, i + k // K
                    wait_alone(pool, loaded[slot], 32 * use + 32)
                    wait_alone(pool, prod1_done, START + K * i + k - K + 1)
                    for j in range(2):
                        nc.gpsimd.indirect_dma_start(msg[:, slot, j, :], None, v["A"], bass.IndirectOffsetOnAxis(
                            ap=rec[:, slot, j:j + 1], axis=0)).then_inc(from_src[slot], 16)

                def destination(i, k):
                    slot, use = k % K, i + k // K
                    wait_alone(pool, from_src[slot], 32 * use + 32)
                    for j in range(2):
                        nc.gpsimd.indirect_dma_start(msg[:, slot, j, :], None, v["B"], bass.IndirectOffsetOnAxis(
                            ap=rec[:, slot, 2 + j:3 + j], axis=0), compute_op=ALU.add).then_inc(from_dst[slot], 16)

                source(0, 0)
                with pool.Fori(0, NI) as i:
                    for k in range(K):
                        source(i, k + 1)
                        destination(i, k)
                source(NI, 1)
                destination(NI, 0)
                destination(NI, 1)

            @block.scalar
            def _(act):
                S = nc.scalar
                for q in (kept, sig_done, h_kept):
                    act.sem_inc(q, START)

                def keep(pt, u):
                    for j in range(2):
                        act.wait_ge(turned, START + u + j + 1)
                        S.activation(pt[:, j, :512], xp[:, j, :], ACT.Copy).then_inc(kept, 1)
                    act.wait_ge(turned, START + u + 3)
                    S.activation(pt[:, :, 512:], yp[:, :, :], ACT.Copy).then_inc(kept, 1)

                def sigmoids(i, k):
                    q = k % 2
                    act.wait_ge(s1_done, START + K * i + k + 1)
                    act.wait_ge(prod2_done, START + K * i + k - 1)
                    S.activation(a_sb[:, q], op[:, :, :CS], ACT.Copy)
                    S.activation(sig[:, q], op[:, :, CS:160], ACT.Sigmoid).then_inc(sig_done, 1)

                keep(pt1, 0)
                sigmoids(0, 0)
                act.wait_ge(s1_done, START + 1)
                keep(pt1, 3)
                act.wait_ge(ones, 1)
                with act.Fori(0, NI) as i:
                    for k in range(K):
                        u = 6 * (K * i + k) + 6
                        act.wait_ge(h_done, START + K * i + k)
                        keep(pt2, u)
                        sigmoids(i, k + 1)
                        act.wait_ge(h_done, START + K * i + k + 1)
                        act.wait_ge(stored[k], 16 * i)
                        S.activation(hs[:, k, :, :, :HW], hp[:, :, :D].rearrange("p j (h w) -> p j h w", h=HEADS),
                                     ACT.Copy).then_inc(h_kept, 1)
                        keep(pt1, u + 3)

            @block.tensor
            def _(pe):
                T = nc.tensor
                for q in (w_done, turned, s1_done, h_done):
                    pe.sem_inc(q, START)

                def weights(i, k):
                    slot = k % K
                    pe.wait_ge(loaded[slot], 32 * (i + k // K) + 32)
                    pe.wait_ge(prod1_done, START + K * i + k - 1)
                    for j in range(2):
                        last = T.matmul(wp[:, k % 2, j * WN1:(j + 1) * WN1], es[:, slot, j * P:(j + 1) * P], W("w_rbf"),
                                        start=True, stop=True)
                    last.then_inc(w_done, 1)

                def turn(prod, u):
                    for j in range(2):
                        pe.wait_ge(kept, START + u + j - 2)
                        for c in range(4):
                            last = T.transpose(xp[:, j, c * P:(c + 1) * P], prod[:, j, c * P:(c + 1) * P], v["ident"][:, :])
                        last.then_inc(turned, 1)
                    pe.wait_ge(kept, START + u)
                    for j in range(2):
                        last = T.transpose(yp[:, j, :], prod[:, j, 512:], v["ident"][:, :])
                    last.then_inc(turned, 1)

                def stage1(i, k, u):
                    pe.wait_ge(kept, START + u + 3)
                    pe.wait_ge(op_read, START + K * i + k)
                    pe.wait_ge(sig_done, START + K * i + k)
                    for j in range(2):
                        for c in (3, 4):
                            T.matmul(op[:, j, :320], pt1[:, j, c * P:(c + 1) * P], v["w1c"][:, c - 3, :], start=c == 3, stop=False)
                        for x in range(3):
                            for o in (160 + CV * x, 256 + CV * x) if x < 2 else (160 + CV * x,):
                                last = T.matmul(op[:, j, o:o + CV], pt1[:, j, x * P:(x + 1) * P], v["w1v"][:, :], start=False,
                                                stop=x == 2)
                    last.then_inc(s1_done, 1)

                weights(0, 0)
                weights(0, 1)
                pe.wait_ge(prod1_done, START + 1)
                turn(prod1[:, 0], 0)
                stage1(0, 0, 0)
                weights(0, 2)
                pe.wait_ge(prod1_done, START + 2)
                turn(prod1[:, 1], 3)
                with pe.Fori(0, NI) as i:
                    for k in range(K):
                        u = 6 * (K * i + k) + 6
                        pe.wait_ge(prod2_done, START + K * i + k + 1)
                        turn(prod2[:, k % 2], u)
                        stage1(i, k + 1, u - 3)
                        pe.wait_ge(kept, START + u + 3)
                        pe.wait_ge(h_kept, START + K * i + k)
                        for j in range(2):
                            for c in range(5):
                                last = T.matmul(hp[:, j, :D], pt2[:, j, c * P:(c + 1) * P], v["w2"][:, c, :], start=c == 0, stop=c == 4)
                        last.then_inc(h_done, 1)
                        weights(i, k + 3)
                        pe.wait_ge(prod1_done, START + K * i + k + 3)
                        turn(prod1[:, k % 2], u + 3)

            @block.vector
            def _(dve):
                V = nc.vector
                for q in (prod1_done, prod2_done, op_read):
                    dve.sem_inc(q, START)
                s = Steps(dve, step)
                s.link(V.memset(hs[:, :, :, :, HW:], 1.0))
                dve.sem_inc(ones, 1)
                dve.wait_ge(ones, 1)
                PER1, PER2 = 12, 9
                first = s.n

                three = lambda ap: ap.rearrange("p j (m u) -> p j m u", m=3)
                over = lambda ap, m: ap.unsqueeze(2).broadcast_to([P, 2, m, ap.shape[-1]])

                def terms(out, y, ss, sv, vs, vs_by, vy, c5):
                    ys = lambda a, n: y[:, :, a:a + 3].unsqueeze(3).broadcast_to([P, 2, 3, n])
                    blocks = out[:, :, :384].rearrange("p j (m w) -> p j m w", m=3)
                    return [
                        lambda: V.tensor_tensor(blocks[:, :, :, :CS], over(sv, 3), ys(1, CS), ALU.mult),
                        lambda: V.tensor_tensor(out[:, :, 576:], ss, y[:, :, 0:1].broadcast_to([P, 2, CS]), ALU.mult),
                        lambda: V.tensor_tensor(blocks[:, :, :, CS:96], three(vs), vs_by, ALU.mult),
                        lambda: V.tensor_tensor(three(out[:, :, 384:480]), three(vy), ys(1, CV), ALU.mult),
                        lambda: V.tensor_tensor(blocks[:, :, :, 96:], three(c5[:, :, CV:4 * CV]), ys(3, CV), ALU.mult),
                        lambda: V.tensor_tensor(three(out[:, :, 480:576]), three(c5[:, :, 2 * CV:]), ys(2, CV), ALU.mult),
                    ]

                def layer1(i, k):
                    slot, q = k % K, k % 2
                    y = rec[:, slot, 4:].bitcast(F32).rearrange("p (j c) -> p j c", j=2)
                    m = msg[:, slot]
                    w = wp[:, q, :2 * WN1].rearrange("p (j w) -> p j w", j=2)
                    dve.wait_ge(from_dst[slot], 32 * (i + k // K) + 32)
                    dve.wait_ge(w_done, START + K * i + k + 1)
                    a = s.did(V.tensor_tensor(wy[:, q], w[:, :, 128:160], y[:, :, 0:1].broadcast_to([P, 2, CV]), ALU.mult))
                    b = s.did(V.tensor_tensor(pw[:, q], w[:, :, :2 * CS].rearrange("p j (a u) -> p j a u", a=2),
                                              m[:, :, :CS].unsqueeze(2).broadcast_to([P, 2, 2, CS]), ALU.mult))
                    c = s.did(V.tensor_tensor(three(qv[:, q]), three(m[:, :, CS:D]), over(w[:, :, 160:192], 3), ALU.mult))
                    d = s.did(V.tensor_tensor(qc[:, q].rearrange("p j (m u) -> p j m u", m=5),
                                              m[:, :, CS:].rearrange("p j (m u) -> p j m u", m=5), over(w[:, :, 192:], 5), ALU.mult))
                    s.did(V.tensor_copy(yk[:, slot], y))
                    dve.wait_ge(turned, START + 6 * (K * i + k) - 12)
                    t = terms(prod1[:, q], y, pw[:, q, :, 0], pw[:, q, :, 1], m[:, :, CS:D], over(wy[:, q], 3), qv[:, q], qc[:, q])
                    s.after(b)
                    s.did(t[0]())
                    s.did(t[1]())
                    s.did(t[2]())
                    s.after(c)
                    s.did(t[3]())
                    s.after(d)
                    s.did(t[4]())
                    t[5]().then_inc(prod1_done, 1)

                def layer2(i, k):
                    slot, q = k % K, k % 2
                    y = yk[:, slot]
                    dve.wait_ge(sig_done, START + K * i + k + 1)
                    a = s.did(V.tensor_tensor(vg[:, q].rearrange("p j (m u) -> p j m u", m=5),
                                              op[:, :, 160:320].rearrange("p j (m u) -> p j m u", m=5),
                                              over(sig[:, q, :, CS:], 5), ALU.mult))
                    V.scalar_tensor_tensor(lr[:, q], op[:, :, :CS], 0.2, a_sb[:, q], ALU.mult, ALU.max).then_inc(op_read, 1)
                    val = sig[:, q, :, :CS]
                    dve.wait_ge(turned, START + 6 * (K * i + k) - 3)
                    t = terms(prod2[:, q], y, val, val, vg[:, q, :, :96], y[:, :, 0:1].unsqueeze(3).broadcast_to([P, 2, 3, CV]),
                              vg[:, q, :, :96], vg[:, q])
                    s.did(t[0]())
                    s.did(t[1]())
                    s.after(a)
                    s.did(t[2]())
                    dve.wait_ge(op_read, START + K * i + k + 1)
                    b = s.did(V.tensor_tensor(la[:, q], lr[:, q], W("alpha_dot").unsqueeze(1).broadcast_to([P, 2, CS]), ALU.mult))
                    s.did(t[3]())
                    s.did(t[4]())
                    s.after(b)
                    s.did(V.tensor_reduce(v["logit"][:, bass.ds(2 * (K * i + k), 2), :],
                                          la[:, q].rearrange("p j (h a) -> p j h a", h=HEADS), AX.X, ALU.add))
                    t[5]().then_inc(prod2_done, 1)

                s.base = 0
                layer1(0, 0)
                layer1(0, 1)
                first = s.n
                per = 18
                with dve.Fori(0, NI) as i:
                    s.n = 0
                    s.base = first + K * per * i
                    for k in range(K):
                        layer2(i, k)
                        layer1(i, k + 2)
                    assert s.n == K * per, s.n


def softmax(nc, v):
    ident, logit = v["ident"], v["logit"]
    seg_open, seg_shut = v["seg_open"], v["seg_shut"]
    with Stage(nc, "softmax") as st:
        a = st.sb("a", [P, NC, HEADS, P])
        f = st.sb("f", [P, NC, HEADS, P])
        cols = st.sb("cols", [P, 4, NC, HEADS])
        lines = st.sb("lines", [HEADS, 4, NTC])
        block_ = st.sb("block", [HEADS, 2, NTC])
        run = st.sb("run", [HEADS, 2, NTC])
        given = block_
        back = st.sb("back", [P, 2, NC, HEADS])
        tp = st.ps("tp", [P, 2, 512])
        cp = st.ps("cp", [HEADS, 2, 512])
        bp = st.ps("bp", [P, 2, NC, HEADS])
        turned, kept, tails, cturned, ckept = (st.sem(n) for n in ("turned", "kept", "tails", "cturned", "ckept"))
        carried, bturned, bkept, lowered = (st.sem(n) for n in ("carried", "bturned", "bkept", "lowered"))
        exped, step = st.sem("exped"), st.sem("step")
        back_turned, written = st.sem("back_turned"), st.sem("written")
        groups = [(q, g) for q in range(4) for g in range(0, NC, 4)]
        width = lambda g: min(4, NC - g)
        with nc.Block() as block:

            @block.tensor
            def _(pe):
                T = nc.tensor
                for c in range(NC):
                    if c >= 2:
                        pe.wait_ge(kept, c - 1)
                    for h in range(HEADS):
                        last = T.transpose(tp[:, c % 2, h * P:(h + 1) * P], logit[:, c * P:(c + 1) * P, h], ident[:, :])
                    last.then_inc(turned, 1)
                pe.wait_ge(tails, 1)
                for n, (q, g) in enumerate(groups):
                    if n >= 2:
                        pe.wait_ge(ckept, n - 1)
                    for c in range(width(g)):
                        last = T.transpose(cp[:, n % 2, c * P:(c + 1) * P], cols[:, q, g + c, :], ident[:, :])
                    last.then_inc(cturned, 1)
                pe.wait_ge(carried, 1)
                for q in range(2):
                    for c in range(NC):
                        last = T.transpose(bp[:, q, c, :], given[:, q, c * P:(c + 1) * P], ident[:HEADS, :HEADS])
                last.then_inc(bturned, 1)
                for c in range(NC):
                    pe.wait_ge(exped, c + 1)
                    if c >= 2:
                        pe.wait_ge(written, c - 1)
                    for h in range(HEADS):
                        last = T.transpose(tp[:, c % 2, h * P:(h + 1) * P], a[:, c, h, :], ident[:, :])
                    last.then_inc(back_turned, 1)

            @block.scalar
            def _(act):
                S = nc.scalar
                for c in range(NC):
                    act.wait_ge(turned, c + 1)
                    S.activation(a[:, c].rearrange("p h e -> p (h e)"), tp[:, c % 2, :], ACT.Copy).then_inc(kept, 1)
                for n, (q, g) in enumerate(groups):
                    act.wait_ge(cturned, n + 1)
                    S.activation(lines[:, q, g * P:(g + width(g)) * P], cp[:, n % 2, :width(g) * P], ACT.Copy).then_inc(ckept, 1)
                act.wait_ge(bturned, 1)
                S.activation(back[:, :, :, :], bp[:, :, :, :], ACT.Copy).then_inc(bkept, 1)
                for c in range(NC):
                    act.wait_ge(lowered, c + 1)
                    S.activation(a[:, c], f[:, c], ACT.Exp).then_inc(exped, 1)
                for c in range(NC):
                    act.wait_ge(back_turned, c + 1)
                    S.activation(logit[:, c * P:(c + 1) * P, :].rearrange("p t h -> p h t"),
                                 tp[:, c % 2, :].rearrange("p (h t) -> p h t", h=HEADS), ACT.Copy).then_inc(written, 1)
                act.wait_ge(written, NC)

            @block.vector
            def _(dve):
                V = nc.vector
                s = Steps(dve, step)
                peak = logit[:, :, :].rearrange("p t h -> p (t h)").rearrange("p (c h e) -> p c h e", c=NC, h=HEADS)
                for c in range(NC):
                    dve.wait_ge(kept, c + 1)
                    for h in range(HEADS):
                        s.did(V.tensor_tensor_scan(f[:, c, h], seg_open[:, c], a[:, c, h], -BIG, ALU.add, ALU.max))
                s.after(s.n)
                for c in range(NC):
                    for h in range(HEADS):
                        s.did(V.tensor_tensor_scan(peak[:, c, h, ::-1], seg_shut[:, c, ::-1], f[:, c, h, ::-1], -BIG, ALU.add, ALU.max))
                s.after(s.n)
                s.did(V.tensor_copy(cols[:, 0], f[:, :, :, P - 1]))
                s.did(V.tensor_copy(cols[:, 1], peak[:, :, :, 0]))
                s.did(V.tensor_copy(cols[:, 2], v["one_seg"][:, :, :]))
                s.after(s.n)
                V.tensor_copy(cols[:, 3], v["goes_on"][:, :, :]).then_inc(tails, 1)
                dve.wait_ge(ckept, len(groups))
                tail, head, one, on = (lines[:, q] for q in range(4))
                ahead, behind = block_[:, 0], block_[:, 1]
                s.did(V.memset(block_[:, 1, NTC - 1:], 0.0))
                s.did(V.tensor_tensor(ahead, one, on, ALU.mult))
                s.link(V.tensor_tensor(behind[:, :NTC - 1], one[:, :NTC - 1], on[:, 1:], ALU.mult))
                s.link(V.tensor_scalar(block_[:, :, :], block_[:, :, :], 1.0, BIG, ALU.subtract, ALU.mult))
                s.did(V.tensor_tensor_scan(run[:, 0], ahead, tail, -BIG, ALU.add, ALU.max))
                s.did(V.tensor_tensor_scan(run[:, 1, ::-1], behind[:, ::-1], head[:, ::-1], -BIG, ALU.add, ALU.max))
                s.after(s.n)
                s.did(V.memset(given[:, 0, 0:1], -BIG))
                s.did(V.memset(given[:, 1, NTC - 1:], -BIG))
                s.link(V.tensor_scalar(lines[:, 2], on, 1.0, BIG, ALU.subtract, ALU.mult))
                s.did(V.tensor_tensor(given[:, 0, 1:], run[:, 0, :NTC - 1], lines[:, 2, 1:], ALU.add))
                s.after(s.n)
                V.tensor_tensor(given[:, 1, :NTC - 1], run[:, 1, 1:], lines[:, 2, 1:], ALU.add).then_inc(carried, 1)
                dve.wait_ge(bkept, 1)
                for c in range(NC):
                    for h in range(HEADS):
                        s.did(V.scalar_tensor_tensor(f[:, c, h], v["not_first"][:, c], back[:, 0, c, h:h + 1], peak[:, c, h],
                                                     ALU.add, ALU.max))
                    s.after(s.n)
                    for h in range(HEADS):
                        s.did(V.scalar_tensor_tensor(peak[:, c, h], v["not_last"][:, c], back[:, 1, c, h:h + 1], f[:, c, h],
                                                     ALU.add, ALU.max))
                    s.after(s.n)
                    V.tensor_tensor(f[:, c], a[:, c], peak[:, c], ALU.subtract).then_inc(lowered, 1)


def edges2(nc, v):
    iota, tabs, rowidx = v["iota"], v["tabs"], v["rowidx"]
    with Stage(nc, "edges2") as st:
        hs = st.sb("hs", [P, K, 2 * HR])
        vals = st.sb("vals", [P, 2, 2, HR])
        onehot = st.sb("onehot", [P, 2, 2, P])
        carry = st.sb("carry", [P, 2, 2])
        acc = st.sb("acc", [P, K, HR])
        rows = st.sb("rows", [P, K], I32)
        sums = st.ps("sums", [P, 2, 512])
        loaded = [st.sem(f"loaded{k}") for k in range(K)]
        scattered = [st.sem(f"scattered{k}") for k in range(K)]
        vals_done, sum_done, kept, step = (st.sem(n) for n in ("vals_done", "sum_done", "kept", "step"))
        cleared = st.sem("cleared")
        with nc.Block() as block:

            @block.sync
            def _(sp):
                with sp.Fori(0, NI) as i:
                    for k in range(K):
                        sp.wait_ge(vals_done, START + K * i + k - K + 1)
                        sp.dma_start(hs[:, k, :], v["H"][bass.ds(K * i + k, 1)].rearrange("o p w -> (o p) w")).then_inc(loaded[k], 16)

            @block.gpsimd
            def _(pool):
                with pool.Fori(0, NI) as i:
                    for k in range(K):
                        scatter(nc, pool, v["T1"], acc, rows, HR, kept, scattered, i, k)
                scatter_end(pool, scattered)

            @block.scalar
            def _(act):
                act.sem_inc(kept, START)
                with act.Fori(0, NI) as i:
                    for k in range(K):
                        for j in range(2):
                            slot = 2 * (k % 2) + j
                            act.wait_ge(sum_done, START + 2 * (K * i + k) + j + 1)
                            act.wait_ge(scattered[slot], 16 * (2 * i + k // 2))
                            nc.scalar.activation(rows[:, slot:slot + 1], rowidx[:, bass.ds(2 * (K * i + k) + j, 1)], ACT.Copy)
                            nc.scalar.activation(acc[:, slot, :], sums[:, j, :HR], ACT.Copy).then_inc(kept, 1)

            @block.tensor
            def _(pe):
                pe.sem_inc(sum_done, START)
                pe.wait_ge(cleared, 1)
                with pe.Fori(0, NI) as i:
                    for k in range(K):
                        pe.wait_ge(vals_done, START + K * i + k + 1)
                        sum_segments(nc, pe, onehot, vals, carry, acc, sums, HR, kept, sum_done, i, k)

            @block.vector
            def _(dve):
                V = nc.vector
                dve.sem_inc(vals_done, START)
                V.memset(acc[:, :, :], 0.0).then_inc(cleared, 1)
                with dve.Fori(0, NI) as i:
                    for k in range(K):
                        q, n = k % 2, 2 * (K * i + k)
                        dve.wait_ge(loaded[k], 16 * i + 16)
                        dve.wait_ge(sum_done, START + 2 * (K * i + k - 2) + 2)
                        V.tensor_tensor(onehot[:, q], tabs[:, 0, bass.ds(n, 2)].unsqueeze(2).broadcast_to([P, 2, P]),
                                        iota[:, :].unsqueeze(1).broadcast_to([P, 2, P]), ALU.is_equal)
                        V.tensor_copy(carry[:, q], tabs[:, 2, bass.ds(n, 2)])
                        V.tensor_tensor(vals[:, q].rearrange("p j (h w) -> p j h w", h=HEADS),
                                        hs[:, k].rearrange("p (j h w) -> p j h w", j=2, h=HEADS),
                                        v["logit"][:, bass.ds(n, 2), :].unsqueeze(3).broadcast_to([P, 2, HEADS, HW + 1]),
                                        ALU.mult).then_inc(vals_done, 1)


def nodes2(nc, v):
    W, ident = v["W"], v["ident"]
    rows_of = lambda t: t.rearrange("(b j p) w -> b p j w", j=2, p=P)
    t3, x3, o3 = rows_of(v["T1"]), rows_of(v["X1"]), rows_of(v["out"])
    at = lambda t, b: t[bass.ds(b, 1)].rearrange("o p j w -> (o p) j w")
    with Stage(nc, "nodes2") as st:
        ts, xs = st.sb("ts", [P, 2, HR]), st.sb("xs", [P, 2, D])
        den, rden = st.sb("den", [P, 2, HEADS]), st.sb("rden", [P, 2, HEADS])
        agg, y, os = st.sb("agg", [P, 2, D]), st.sb("y", [P, 2, D]), st.sb("os", [P, 2, D])
        aT = st.sb("aT", [80, 2, 256])
        stats, mv = st.sb("stats", [P, 2, 6]), st.sb("mv", [P, 2, 2])
        var, root, rstd = (st.sb(n, [P, 2]) for n in ("var", "root", "rstd"))
        tp, pp = st.ps("tp", [80, 2, 256]), st.ps("pp", [P, 2, 256])
        sem = {n: st.sem(n) for n in ("loaded", "agg_done", "turned", "kept", "product", "varied", "rooted", "done", "stored", "step")}
        with nc.Block() as block:

            @block.sync
            def _(sp):
                with sp.Fori(0, NB) as b:
                    sp.wait_ge(sem["done"], b)
                    sp.dma_start(ts[:, :, :], at(t3, b)).then_inc(sem["loaded"], 16)
                    sp.dma_start(xs[:, :, :], at(x3, b)).then_inc(sem["loaded"], 16)
                    sp.wait_ge(sem["done"], b + 1)
                    sp.dma_start(at(o3, b), os[:, :, :]).then_inc(sem["stored"], 16)
                sp.wait_ge(sem["stored"], 16 * NB)

            @block.tensor
            def _(pe):
                T = nc.tensor
                with pe.Fori(0, NB) as b:
                    pe.wait_ge(sem["agg_done"], b + 1)
                    for j in range(2):
                        for c in range(2):
                            last = T.transpose(tp[:, j, c * P:(c + 1) * P], agg[:, j, 80 * c:80 * c + 80], ident[:, :])
                    last.then_inc(sem["turned"], 1)
                    pe.wait_ge(sem["kept"], b + 1)
                    for j in range(2):
                        for c in range(2):
                            last = T.matmul(pp[:, j, :D], aT[:, j, c * P:(c + 1) * P], W(f"wp{c}"), start=c == 0, stop=c == 1)
                    last.then_inc(sem["product"], 1)

            @block.scalar
            def _(act):
                with act.Fori(0, NB) as b:
                    act.wait_ge(sem["turned"], b + 1)
                    nc.scalar.activation(aT[:, :, :], tp[:, :, :], ACT.Copy).then_inc(sem["kept"], 1)
                    act.wait_ge(sem["varied"], b + 1)
                    nc.scalar.activation(root[:, :], var[:, :], ACT.Sqrt).then_inc(sem["rooted"], 1)

            @block.vector
            def _(dve):
                V = nc.vector
                s = Steps(dve, sem["step"])
                PER = 8
                with dve.Fori(0, NB) as b:
                    s.n, s.base = 0, PER * b

                    def rooted(ins):
                        ins.then_inc(sem["varied"], 1)
                        dve.wait_ge(sem["rooted"], b + 1)

                    dve.wait_ge(sem["loaded"], 32 * b + 32)
                    heads = ts[:, :, :].rearrange("p j (h w) -> p j h w", h=HEADS)
                    s.link(V.tensor_scalar(den[:, :, :], heads[:, :, :, HW], 1e-16, None, ALU.add))
                    s.link(V.reciprocal(rden[:, :, :], den[:, :, :]))
                    V.tensor_tensor(agg[:, :, :].rearrange("p j (h w) -> p j h w", h=HEADS), heads[:, :, :, :HW],
                                    rden[:, :, :].unsqueeze(3).broadcast_to([P, 2, HEADS, HW]), ALU.mult).then_inc(sem["agg_done"], 1)
                    dve.wait_ge(sem["product"], b + 1)
                    s.link(V.scalar_tensor_tensor(y[:, :, :], xs[:, :, :], 2.0, pp[:, :, :D], ALU.mult, ALU.add))
                    layer_norm(V, s, rooted, stats, mv, var, rstd, y, 2)
                    s.link(V.reciprocal(rstd[:, :], root[:, :]))
                    dve.wait_ge(sem["stored"], 16 * b)
                    V.tensor_scalar(os[:, 0, :], y[:, 0, :], mv[:, 0, 0:1], rstd[:, 0:1], ALU.subtract, ALU.mult)
                    V.tensor_scalar(os[:, 1, :], y[:, 1, :], mv[:, 1, 0:1], rstd[:, 1:2], ALU.subtract, ALU.mult).then_inc(sem["done"], 1)
                    assert s.n == PER, s.n


def weight_blocks(w):
    z = lambda *s: np.zeros(s, np.float32)
    b = {"fc1": w["Wfc1"], "fc2": w["Wfc2"], "l1_0": w["Wl1_0"], "sc0": w["Wsc0"]}
    b["l1_1"], b["sc1"] = z(96, 96), z(96, 96)
    for m in range(3):
        b["l1_1"][m::3, CV * m:CV * m + CV] = w["Wl1_1"]
        b["sc1"][m::3, m::3] = w["Wsc1"]
    b["l2s"] = np.concatenate([w["Wl2_s"], w["Wa"]], axis=1)
    b["l2v"] = w["Wl2_v"]
    b["w_rbf"] = w["W_rbf"]
    for side in ("src", "dst"):
        b["ws_" + side] = w["Ws_" + side]
        b["wv_" + side] = z(96, 5 * CV)
        for m in range(5):
            b["wv_" + side][m % 3::3, CV * m:CV * m + CV] = w["Wv_" + side]
    b["wv_val"] = w["Wv_val"]
    cross = w["Wv_val"][96:]
    for c in range(2):
        b[f"w1c{c}"], b[f"ws_valT{c}"] = z(P, 320), z(CS, P)
    rows = [[(r, CS, CS + CV) for r in (0, CV, 2 * CV)], [(CS, 0, CS)]]
    for c in range(2):
        for at, lo, hi in rows[c]:
            b[f"w1c{c}"][at:at + hi - lo, :CS] = w["W_alpha"][lo:hi]
            b[f"w1c{c}"][at:at + hi - lo, CS:128] = w["Ws_val"][lo:hi]
            b[f"ws_valT{c}"][:, at:at + hi - lo] = w["Ws_val"][lo:hi].T
    for c, at, x in ((0, 96, 0), (1, 0, 1), (1, CV, 2)):
        for m in (x, x + 3) if x < 2 else (x,):
            b[f"w1c{c}"][at:at + CV, 160 + CV * m:160 + CV * m + CV] = cross
    b["wg"] = w["Wg"]
    head_s = [HW * h + a for h in range(HEADS) for a in range(AS)]
    head_v = [[HW * h + AS + AV * x + a for h in range(HEADS) for a in range(AV)] for x in range(3)]
    sl, vl = w["Ws_vlin"], w["Wv_vlin"]
    two = z(5 * P, D)
    scale = z(5 * P)
    for x in range(3):
        two[P * x:P * x + P, head_v[x]] = vl
        scale[P * x:P * x + P] = np.concatenate([w["w2_sv"], w["w2_vs"], w["w2_vv1"]])
        two[384 + CV * x:384 + CV * x + CV, head_s] = sl[CS:]
        scale[384 + CV * x:384 + CV * x + CV] = w["w2_vv0"]
        two[480 + CV * x:480 + CV * x + CV, head_v[x]] = vl[96:]
        scale[480 + CV * x:480 + CV * x + CV] = w["w2_vv1"]
    two[576:, head_s] = sl[:CS]
    scale[576:] = w["w2_ss"]
    for c in range(5):
        b[f"w2_{c}"] = two[P * c:P * c + P]
    b["w2s"] = scale.reshape(5, P).T
    out = z(D, D)
    out[head_s, :CS] = w["Wps"]
    for x in range(3):
        out[head_v[x], CS + x::3] = w["Wpv"]
    b["wp0"], b["wp1"] = out[:80], out[80:]
    for name, row in (("gamma_s", w["gamma_s"]), ("beta_s", w["beta_s"]), ("gamma_v", w["gamma_v"]), ("alpha_dot", w["alpha_dot"].reshape(-1))):
        b[name] = np.broadcast_to(row, (P, row.shape[0]))
    return b


def constant_columns():
    c = np.ones((P, 9), np.float32)
    c[:, 0] = 96 ** -0.5
    c[CS:96, 0] /= 3 ** 0.5
    c[96:, 1] = 2 ** -0.5
    c[:96, 2], c[96:, 2] = 3 ** -0.5, -(2 ** -0.5)
    c[:CS, 3], c[CS:, 3] = -(2 ** -0.5), 1.0
    for x in range(3):
        c[96:, 4 + x] = 2 ** -0.5
    c[:, 7:9] = c[:, 2:4]
    return c


def kernel(**inputs):
    import numpy as _np
    import concourse.bacc as _bacc
    from concourse import mybir as _mybir
    from concourse.bass_utils import run_bass_kernel_spmd as _run

    g = {k: _np.asarray(a) for k, a in inputs.items()}
    w = {k[7:]: a for k, a in g.items() if k.startswith("L")}
    x = _np.zeros((NN, D), _np.float32)
    x[:N] = g["x"]
    attr = _np.zeros((NN,), _np.float32)
    attr[:N] = g["node_vec1"][:, 0]
    edges = NPL * 2 * P
    src, dst = _np.zeros(edges, _np.int32), _np.full(edges, N, _np.int32)
    src[:E], dst[:E] = g["src"], g["dst"]
    dstp = _np.full(P + 1 + NTC * P + P + 1, N, _np.int32)
    dstp[:P + 1] = -1
    dstp[P + 1:P + 1 + E] = g["dst"]
    es = _np.zeros((FC, edges), _np.float32)
    es[:, :E] = g["edge_attr_16"].T
    sh = _np.zeros((edges, 6), _np.float32)
    sh[:E] = g["edge_attr_4"][:, [0, 1, 2, 3, 1, 2]]
    by_pair = lambda a: a.reshape(NPL, 2, P, -1).transpose(0, 2, 1, 3).reshape(NPL, P, -1)
    meta = _np.concatenate([by_pair(src), by_pair(dst), by_pair(sh.view(_np.int32))], axis=2)
    blocks = weight_blocks(w)
    at = 0
    for name, a in blocks.items():
        W_COLS[name] = (at, a.shape[0], a.shape[1])
        at += a.shape[1]
    wpack = _np.zeros((P, at), _np.float32)
    for name, a in blocks.items():
        o, r, c = W_COLS[name]
        wpack[:r, o:o + c] = a
    ins = {"x": x, "attr": _np.ascontiguousarray(attr.reshape(2 * NB, P).T), "meta": _np.ascontiguousarray(meta),
           "dstp": dstp, "esT": es, "wpack": wpack, "wconst": constant_columns()}
    nc = _bacc.Bacc("TRN2", target_bir_lowering=False, num_devices=1)
    arrays = {f"in_{n}": a for n, a in ins.items()}
    aps = {n: nc.dram_tensor(f"in_{n}", a.shape, _mybir.dt.from_np(a.dtype), kind="ExternalInput").ap() for n, a in ins.items()}
    aps["out"] = nc.dram_tensor("out_nodes", (NN, D), _mybir.dt.float32, kind="ExternalOutput").ap()
    build(nc, **aps)
    r = _run(nc, [arrays], core_ids=[0])
    return r.results[0]["out_nodes"][:N]
```

```python
import concourse.bass as bass
from concourse import mybir
from contextlib import ExitStack
import numpy as np

P = 128
N, E = 12500, 200000
CS, CV = 64, 32
D = CS + 3 * CV
DX = CS + 5 * CV
FC, WN0, WN1 = 16, 192, 224
HEADS, AS, AV = 4, 16, 8
HW = AS + 3 * AV
K = 4
NP = 784
NT = 2 * NP
NI = NP // K
NPL = NP + K
NC = 13
NTC = NC * P
NB = 49
NN = NB * 2 * P
T0W = 4 * 96 + 2
T0I = T0W - 1
HR = HEADS * (HW + 1)
SKIP = 16384
BIG = 1.0e30
START = 16
META = 16
EPS = 1e-5

F32 = mybir.dt.float32
I32 = mybir.dt.int32
BF16 = mybir.dt.bfloat16
ALU = mybir.AluOpType
ACT = mybir.ActivationFunctionType
AX = mybir.AxisListType
W_COLS = {}


def wait_alone(eng, sem, value):
    if not isinstance(value, int):
        value = eng.snap(eng.to_reg(value))
    eng.wait_ge(sem, 0)
    eng.wait_ge(sem, value)


class Steps:

    def __init__(self, eng, sem):
        self.eng, self.sem, self.n, self.base = eng, sem, 0, 0

    def did(self, ins):
        ins.then_inc(self.sem, 1)
        self.n += 1
        return self.n

    def after(self, n):
        self.eng.wait_ge(self.sem, self.base + n)

    def after_alone(self, n):
        wait_alone(self.eng, self.sem, self.base + n)

    def link(self, ins):
        self.after(self.did(ins))


def build(nc, x, attr, meta, dstp, esT, wpack, wconst, out):
    top = ExitStack()
    dram = lambda name, shape, dt=F32: nc.dram_tensor(name, shape, dt).ap()
    F = dram("F_table", [NN, D])
    T0 = dram("T0_table", [NN, T0W])
    A = dram("A_table", [NN, DX])
    B = dram("B_table", [NN, DX])
    X1 = dram("X1_nodes", [NN, D])
    H = dram("H_messages", [NP, P, 2 * HR])
    T1 = dram("T1_table", [NN, HR])

    with top:
        sb = lambda name, shape, dt=F32: top.enter_context(nc.sbuf_tensor(name, shape, dt))
        wt = sb("wt", [P, wpack.shape[1]])
        wc = sb("wc", [P, wconst.shape[1]])
        ident = sb("ident", [P, P])
        iota = sb("iota", [P, P])
        tabs = sb("tabs", [P, 3, NTC])
        logit = sb("logit", [P, NTC, HEADS])
        rowidx = sb("rowidx", [P, NT], I32)
        attr_s = sb("attr_s", [P, 2 * NB])
        w1v = sb("w1v", [P, CV])
        w1s = sb("w1s", [P, 160])
        w2v = sb("w2v", [P, CV])
        w2s = sb("w2s", [P, CS])
        seg_open = sb("seg_open", [P, NC, P])
        seg_shut = sb("seg_shut", [P, NC, P])
        not_first = sb("not_first", [P, NC, P])
        not_last = sb("not_last", [P, NC, P])
        one_seg = sb("one_seg", [P, NC, HEADS])
        goes_on = sb("goes_on", [P, NC, HEADS])
        W = lambda name: wt[:W_COLS[name][1], W_COLS[name][0]:W_COLS[name][0] + W_COLS[name][2]]
        C = lambda j: wc[:, j:j + 1]

        prep(nc, locals())
        nodes0(nc, locals())
        edges0(nc, locals())
        nodes1(nc, locals())
        edges1(nc, locals())
        softmax(nc, locals())
        edges2(nc, locals())
        nodes2(nc, locals())


class Stage:

    def __init__(self, nc, name):
        self.nc, self.name, self.stack = nc, name, ExitStack()

    def __enter__(self):
        return self

    def __exit__(self, *a):
        self.stack.close()

    def sb(self, name, shape, dt=F32):
        return self.stack.enter_context(self.nc.sbuf_tensor(f"{self.name}_{name}", shape, dt))

    def ps(self, name, shape, dt=F32):
        return self.stack.enter_context(self.nc.psum_tensor(f"{self.name}_{name}", shape, dt))

    def sem(self, name):
        return self.stack.enter_context(self.nc.semaphore(f"{self.name}_{name}"))


def node_pairs(table):
    return table.rearrange("(b j p) w -> b p j w", j=2, p=P)


def pair_at(pairs, m):
    return pairs[bass.ds(m, 1)].rearrange("o p j w -> (o p) j w")


def prep(nc, v):
    wt, wc, ident, iota, tabs, logit = v["wt"], v["wc"], v["ident"], v["iota"], v["tabs"], v["logit"]
    W, C = v["W"], v["C"]
    w1v, w1s, w2v, w2s = v["w1v"], v["w1s"], v["w2v"], v["w2s"]
    dstp = v["dstp"]
    with Stage(nc, "prep") as st:
        shifts = [0, -1, 1, -P, -P - 1]
        four = logit[:, :, :].bitcast(I32).rearrange("p t h -> p (t h)").rearrange("p (k c e) -> p k c e", k=4, e=P)
        fifth = st.sb("fifth", [P, NC, P], I32)
        ints = [four[:, k] for k in range(4)] + [fifth[:, :, :]]
        dst = st.sb("dst", [P, 5, NC, P])
        opens, opens_before, ends = v["seg_open"], v["not_first"], v["seg_shut"]
        last_rank = st.sb("last_rank", [P, NC])
        byt = st.sb("byt", [P, 3, NC, P])
        zero = st.sb("zero", [P, 512])
        cont = st.sb("cont", [P, NC])
        single = st.sb("single", [P, NC])
        tp = st.ps("tp", [P, 2, 512])
        gp = st.ps("gp", [96, CV])
        loaded, made, built = st.sem("loaded"), st.sem("made"), st.sem("built")
        turned, kept, cleared, step = st.sem("turned"), st.sem("kept"), st.sem("cleared"), st.sem("step")
        gates, zeroed = st.sem("gates"), st.sem("zeroed")
        T0, T1 = v["T0"], v["T1"]
        jobs = [(k, c) for k in range(3) for c in range(NC)]
        batches = [jobs[a:a + 4] for a in range(0, len(jobs), 4)]
        with nc.Block() as block:

            @block.sync
            def _(sp):
                sp.dma_start(wt[:, :], v["wpack"]).then_inc(loaded, 16)
                sp.dma_start(wc[:, :], v["wconst"]).then_inc(loaded, 16)
                sp.dma_start(v["attr_s"][:, :], v["attr"]).then_inc(loaded, 16)
                for k, s in enumerate(shifts):
                    src = dstp[P + 1 + s:P + 1 + s + NTC * P].rearrange("(c p e) -> p c e", p=P, e=P)
                    sp.dma_start(ints[k], src).then_inc(loaded, 16)
                sp.wait_ge(zeroed, 1)
                n = 0
                for table, width in ((T0, T0W), (T1, HR)):
                    flat = table.rearrange("n w -> (n w)").rearrange("(q p w) -> q p w", p=P, w=width)
                    for q in range(2 * NB):
                        sp.dma_start(flat[q], zero[:, :width]).then_inc(cleared, 16)
                        n += 16
                sp.wait_ge(cleared, n)

            @block.gpsimd
            def _(pool):
                nc.gpsimd.memset(ident[:, :], 0.0).then_inc(made, 1)
                nc.gpsimd.iota(iota[:, :], [[1, P]], base=0, channel_multiplier=0,
                               allow_small_or_imprecise_dtypes=True).then_inc(made, 1)
                pool.wait_ge(made, 2)
                nc.gpsimd.affine_select(out=ident[:, :], in_=ident[:, :], compare_op=ALU.not_equal, fill=1.0,
                                        base=0, pattern=[[-1, P]], channel_multiplier=1).then_inc(made, 1)

            @block.vector
            def _(dve):
                V = nc.vector
                s = Steps(dve, step)
                V.memset(zero[:, :], 0.0).then_inc(zeroed, 1)
                dve.wait_ge(loaded, 16 * 8)
                dve.wait_ge(made, 3)
                for name, const in (("fc1", 1 / 4), ("fc2", 1 / 8), ("l1_0", 1 / 8), ("sc0", 1 / 8),
                                    ("l1_1", CV ** -0.5), ("sc1", CV ** -0.5), ("l2v", 96 ** -0.5)):
                    s.link(V.tensor_scalar(W(name), W(name), const, None, ALU.mult))
                s.link(V.tensor_scalar(W("l2s"), W("l2s"), wc[:96, 0:1], None, ALU.mult))
                s.link(V.tensor_scalar(w1v[:, :], W("wv_val"), C(1), None, ALU.mult))
                s.did(V.memset(w1s[:, :], 0.0))
                s.link(V.memset(w2s[:, :], 0.0))
                s.link(V.tensor_scalar(w1s[:96, :128], W("w1s"), wc[:96, 2:3], None, ALU.mult))
                s.link(V.tensor_scalar(w2v[:, :], W("wv_vlin"), C(1), W("w2_v"), ALU.mult, ALU.mult))
                s.link(V.tensor_scalar(w2s[:96, :], W("ws_vlin"), wc[:96, 2:3], W("w2_s"), ALU.mult, ALU.mult))
                dve.wait_ge(gates, 1)
                s.link(V.tensor_scalar(w1s[:96, 128:], gp[:, :], wc[:96, 2:3], None, ALU.mult))
                for k in range(5):
                    s.did(V.tensor_copy(dst[:, k], ints[k]))
                s.after(s.n)
                s.did(V.memset(logit[:, NT:, :], 0.0))
                this, before, behind, tile_before, before_that = (dst[:, k] for k in range(5))
                s.did(V.tensor_tensor(opens[:, :, :], this, before, ALU.not_equal))
                s.did(V.tensor_tensor(opens_before[:, :, :], tile_before, before_that, ALU.not_equal))
                s.did(V.tensor_tensor(ends[:, :, :], this, behind, ALU.not_equal))
                s.link(V.tensor_tensor(cont[:, :], this[:, :, 0], before[:, :, 0], ALU.is_equal))
                s.did(V.memset(opens[:, :, 0:1], 0.0))
                s.link(V.memset(opens_before[:, :, 0:1], 0.0))
                for c in range(NC):
                    s.did(V.tensor_tensor_scan(byt[:, 0, c], opens[:, c], zero[:, :P], 0.0, ALU.add, ALU.add))
                    s.did(V.tensor_tensor_scan(byt[:, 2, c], opens_before[:, c], zero[:, :P], 0.0, ALU.add, ALU.add))
                s.link(V.scalar_tensor_tensor(byt[:, 1], this, float(-SKIP), ends[:, :, :], ALU.add, ALU.mult))
                s.link(V.tensor_copy(last_rank[:, :], byt[:, 2, :, P - 1]))
                for c in range(NC):
                    s.did(V.tensor_scalar(byt[:, 2, c], iota[:, :], last_rank[:, c:c + 1], cont[:, c:c + 1],
                                          ALU.is_equal, ALU.mult))
                rank = byt[:, 0]
                s.did(V.tensor_scalar(opens[:, :, :], opens[:, :, :], -BIG, None, ALU.mult))
                s.did(V.tensor_scalar(ends[:, :, :], ends[:, :, :], -BIG, None, ALU.mult))
                s.did(V.tensor_scalar(v["not_first"][:, :, :], rank, 0.0, -BIG, ALU.not_equal, ALU.mult))
                for c in range(NC):
                    s.did(V.tensor_scalar(v["not_last"][:, c], rank[:, c], rank[:, c, P - 1:P], -BIG, ALU.not_equal, ALU.mult))
                s.link(V.tensor_scalar(single[:, :], rank[:, :, P - 1], 0.0, None, ALU.is_equal))
                s.did(V.memset(v["seg_open"][:, :, 0:1], -BIG))
                s.did(V.memset(v["seg_shut"][:, :, P - 1:P], -BIG))
                s.did(V.tensor_copy(v["one_seg"][:, :, :], single[:, :].unsqueeze(2).broadcast_to([P, NC, HEADS])))
                V.tensor_copy(v["goes_on"][:, :, :], cont[:, :].unsqueeze(2).broadcast_to([P, NC, HEADS])).then_inc(built, 1)

            @block.tensor
            def _(pe):
                pe.wait_ge(loaded, 16 * 8)
                nc.tensor.matmul(gp[:, :], W("ws_valT"), W("wg"), start=True, stop=True).then_inc(gates, 1)
                pe.wait_ge(made, 3)
                pe.wait_ge(built, 1)
                for b, batch in enumerate(batches):
                    if b >= 2:
                        pe.wait_ge(kept, b - 1)
                    for q, (k, c) in enumerate(batch):
                        last = nc.tensor.transpose(tp[:, b % 2, q * P:(q + 1) * P], byt[:, k, c], ident[:, :])
                    last.then_inc(turned, 1)

            @block.scalar
            def _(act):
                flat = tabs[:, :, :].rearrange("p k t -> p (k t)")
                for b, batch in enumerate(batches):
                    act.wait_ge(turned, b + 1)
                    w = len(batch) * P
                    nc.scalar.activation(flat[:, b * 512:b * 512 + w], tp[:, b % 2, :w], ACT.Copy).then_inc(kept, 1)
                act.wait_ge(kept, len(batches))


def nodes0(nc, v):
    W, ident = v["W"], v["ident"]
    x3, f3 = node_pairs(v["x"]), node_pairs(v["F"])
    with Stage(nc, "nodes0") as st:
        xs = st.sb("xs", [P, 2, 2, D])
        xT = st.sb("xT", [P, 2, 2, 256])
        fs = st.sb("fs", [P, 2, 2, D])
        tp, fp = st.ps("tp", [P, 2, 256]), st.ps("fp", [P, 2, D])
        loaded = [st.sem(f"loaded{g}") for g in range(2)]
        stored = [st.sem(f"stored{g}") for g in range(2)]
        turned, kept, product, scaled = (st.sem(n) for n in ("turned", "kept", "product", "scaled"))
        with nc.Block() as block:

            @block.sync
            def _(sp):
                for g in range(2):
                    sp.sem_inc(stored[g], START)
                    sp.dma_start(xs[:, g], pair_at(x3, g)).then_inc(loaded[g], 16)

                def store(m, g):
                    sp.wait_ge(scaled, START + 2 * m + 2)
                    sp.dma_start(pair_at(f3, m), fs[:, g]).then_inc(stored[g], 16)

                def load(m, g):
                    sp.wait_ge(turned, m - 1)
                    sp.dma_start(xs[:, g], pair_at(x3, m)).then_inc(loaded[g], 16)

                with sp.Fori(0, (NB - 3) // 2) as h:
                    for g in range(2):
                        load(2 * h + g + 2, g)
                        store(2 * h + g, g)
                load(NB - 1, (NB - 1) % 2)
                for m in range(NB - 3, NB):
                    store(m, m % 2)
                for g in range(2):
                    sp.wait_ge(stored[g], START + 16 * ((NB + 1 - g) // 2))

            @block.tensor
            def _(pe):
                def turn(m, g, use):
                    pe.wait_ge(loaded[g], 16 * use + 16)
                    wait_alone(pe, kept, START + m)
                    for j in range(2):
                        nc.tensor.transpose(tp[:CS, j, :P], xs[:, g, j, :CS], ident[:, :])
                        last = nc.tensor.transpose(tp[:96, j, P:], xs[:, g, j, CS:], ident[:, :])
                    last.then_inc(turned, 1)

                def multiply(m, g):
                    pe.wait_ge(kept, START + m + 1)
                    pe.wait_ge(scaled, START + 2 * m)
                    for j in range(2):
                        nc.tensor.matmul(fp[:, j, :CS], xT[:CS, g, j, :P], W("l1_0"), start=True, stop=True)
                        last = nc.tensor.matmul(fp[:, j, CS:], xT[:96, g, j, P:], W("l1_1"), start=True, stop=True)
                    last.then_inc(product, 1)

                turn(0, 0, 0)
                with pe.Fori(0, NB // 2) as h:
                    for g in range(2):
                        turn(2 * h + g + 1, 1 - g, h + g)
                        multiply(2 * h + g, g)
                multiply(NB - 1, 0)

            @block.scalar
            def _(act):
                act.sem_inc(kept, START)
                act.sem_inc(scaled, START)
                S = nc.scalar

                def keep(m, g):
                    act.wait_ge(turned, m + 1)
                    S.activation(xT[:CS, g, :, :P], tp[:CS, :, :P], ACT.Copy)
                    S.activation(xT[:96, g, :, P:], tp[:96, :, P:], ACT.Copy).then_inc(kept, 1)

                def scale(m, g, use):
                    act.wait_ge(product, m + 1)
                    act.wait_ge(stored[g], START + 16 * use)
                    for j in range(2):
                        S.activation(fs[:, g, j, :], fp[:, j, :], ACT.Copy,
                                     scale=v["attr_s"][:, bass.ds(2 * m + j, 1)]).then_inc(scaled, 1)

                keep(0, 0)
                with act.Fori(0, NB // 2) as h:
                    for g in range(2):
                        keep(2 * h + g + 1, 1 - g)
                        scale(2 * h + g, g, h)
                scale(NB - 1, 0, NB // 2)


def edges0(nc, v):
    W, iota, tabs = v["W"], v["iota"], v["tabs"]
    with Stage(nc, "edges0") as st:
        rec = st.sb("rec", [P, K, META], I32)
        es = st.sb("es", [FC, K, 256])
        feat = st.sb("feat", [P, K, 2, D])
        hT = st.sb("hT", [CS, 2, 256])
        e1y = st.sb("e1y", [P, 2, 2, 96])
        dot = st.sb("dot", [P, 2, 2, CV])
        p01 = st.sb("p01", [P, 2, 2, 2, CS])
        w2y = st.sb("w2y", [P, 2, 2, CV])
        mid = st.sb("mid", [P, 2, 2, T0W])
        onehot = st.sb("onehot", [P, 2, 2, P])
        carry = st.sb("carry", [P, 2, 2])
        acc = st.sb("acc", [P, K, T0W])
        rows = st.sb("rows", [P, K], I32)
        hp, wp = st.ps("hp", [CS, 2, 512]), st.ps("wp", [P, 2, 512])
        sp_ = st.ps("sums", [P, 2, 512])
        loaded = [st.sem(f"loaded{k}") for k in range(K)]
        gathered = [st.sem(f"gathered{k}") for k in range(K)]
        scattered = [st.sem(f"scattered{k}") for k in range(K)]
        h_done, silu_done, w_done = st.sem("h_done"), st.sem("silu_done"), st.sem("w_done")
        mid_done, sum_done, kept, step = st.sem("mid_done"), st.sem("sum_done"), st.sem("kept"), st.sem("step")
        ones = st.sem("ones")
        y = [rec[:, k, 4:].bitcast(F32).rearrange("p (j c) -> p j c", j=2) for k in range(K)]
        with nc.Block() as block:

            @block.sync
            def _(sp):
                load = lambda i, k: load_pair(sp, v, rec, es, loaded, gathered, h_done, mid_done, i, k)
                for k in range(K):
                    load(0, k)
                with sp.Fori(1, NPL // K) as i:
                    for k in range(K):
                        load(i, k)
                for k in range(K):
                    sp.wait_ge(loaded[k], 32 * (NPL // K))
                    sp.wait_ge(gathered[k], 32 * (NI + (k < 3)))

            @block.gpsimd
            def _(pool):
                def gather(i, k):
                    slot, use = k % K, i + k // K
                    wait_alone(pool, loaded[slot], 32 * use + 32)
                    wait_alone(pool, mid_done, START + K * i + k - K + 1)
                    for j in range(2):
                        nc.gpsimd.indirect_dma_start(feat[:, slot, j, :], None, v["F"], bass.IndirectOffsetOnAxis(
                            ap=rec[:, slot, j:j + 1], axis=0)).then_inc(gathered[slot], 16)

                for k in range(3):
                    gather(0, k)
                with pool.Fori(0, NI) as i:
                    for k in range(K):
                        gather(i, k + 3)
                        scatter(nc, pool, v["T0"], acc, rows, T0W, kept, scattered, i, k)
                scatter_end(pool, scattered)

            @block.scalar
            def _(act):
                act.sem_inc(silu_done, START)
                act.sem_inc(kept, START)

                def silu(i, k):
                    act.wait_ge(h_done, START + K * i + k + 1)
                    act.wait_ge(w_done, START + K * i + k - 1)
                    nc.scalar.activation(hT[:, k % 2, :], hp[:, k % 2, :256], ACT.Silu).then_inc(silu_done, 1)

                def iteration(i):
                    for k in range(K):
                        silu(i, k + 2)
                        keep_sums(nc, act, sp_, acc, rows, T0W, v["rowidx"], sum_done, kept, scattered, i, k)

                for k in range(2):
                    silu(0, k)
                iteration(0)
                with act.Fori(1, NI) as i:
                    iteration(i)

            @block.tensor
            def _(pe):
                pe.sem_inc(h_done, START)
                pe.sem_inc(w_done, START)
                pe.sem_inc(sum_done, START)

                def hidden(i, k):
                    slot = k % K
                    pe.wait_ge(loaded[slot], 32 * (i + k // K) + 32)
                    pe.wait_ge(silu_done, START + K * i + k - 1)
                    nc.tensor.matmul(hp[:, k % 2, :256], W("fc1"), es[:, slot, :], start=True, stop=True).then_inc(h_done, 1)

                def weights(i, k):
                    pe.wait_ge(silu_done, START + K * i + k + 1)
                    pe.wait_ge(mid_done, START + K * i + k - 1)
                    for j in range(2):
                        last = nc.tensor.matmul(wp[:, k % 2, j * WN0:(j + 1) * WN0], hT[:, k % 2, j * P:(j + 1) * P],
                                                W("fc2"), start=True, stop=True)
                    last.then_inc(w_done, 1)

                hidden(0, 0)
                hidden(0, 1)
                weights(0, 0)
                pe.wait_ge(ones, 1)
                with pe.Fori(0, NI) as i:
                    for k in range(K):
                        hidden(i, k + 2)
                        weights(i, k + 1)
                        pe.wait_ge(mid_done, START + K * i + k + 1)
                        sum_segments(nc, pe, onehot, mid, carry, acc, sp_, T0W, kept, sum_done, i, k)

            @block.vector
            def _(dve):
                V = nc.vector
                dve.sem_inc(mid_done, START)
                s = Steps(dve, step)
                for q in range(2):
                    s.did(V.memset(mid[:, q, :, T0W - 2:T0W - 1], 1.0))
                s.link(V.memset(acc[:, :, :], 0.0))
                dve.sem_inc(ones, 1)
                PER = 12
                first = s.n
                with dve.Fori(0, NI) as i:
                    s.n = 0
                    s.base = first + K * PER * i
                    for k in range(K):
                        slot, q = k, k % 2
                        e0, e1 = feat[:, slot, :, :CS], feat[:, slot, :, CS:].rearrange("p j (m u) -> p j m u", m=3)
                        w = wp[:, q, :2 * WN0].rearrange("p (j w) -> p j w", j=2)
                        ys = y[slot]
                        one = lambda c, n: ys[:, :, c:c + 1].broadcast_to([P, 2, n])
                        three = lambda n: ys[:, :, 1:4].unsqueeze(3).broadcast_to([P, 2, 3, n])
                        row = mid[:, q]
                        scal1 = row[:, :, CS:96]
                        vec = row[:, :, 96:384].rearrange("p j (m w) -> p j m w", m=3)
                        dve.wait_ge(gathered[slot], 32 * i + 32)
                        dve.wait_ge(sum_done, START + 2 * (K * i + k - 2) + 2)
                        a = s.did(V.tensor_tensor(e1y[:, q].rearrange("p j (m u) -> p j m u", m=3), e1, three(CV), ALU.mult))
                        s.did(V.tensor_tensor(onehot[:, q], tabs[:, 0, bass.ds(2 * (K * i + k), 2)].unsqueeze(2).broadcast_to([P, 2, P]),
                                              iota[:, :].unsqueeze(1).broadcast_to([P, 2, P]), ALU.is_equal))
                        s.after(a)
                        b = s.did(V.tensor_tensor(dot[:, q], e1y[:, q, :, :CV], e1y[:, q, :, CV:2 * CV], ALU.add))
                        dve.wait_ge(w_done, START + K * i + k + 1)
                        c = s.did(V.tensor_tensor(p01[:, q], w[:, :, :2 * CS].rearrange("p j (a u) -> p j a u", a=2),
                                                  e0.unsqueeze(2).broadcast_to([P, 2, 2, CS]), ALU.mult))
                        s.after(b)
                        b = s.did(V.tensor_tensor(dot[:, q], dot[:, q], e1y[:, q, :, 2 * CV:], ALU.add))
                        d = s.did(V.tensor_tensor(w2y[:, q], w[:, :, 128:160], one(0, CV), ALU.mult))
                        s.after(c)
                        s.did(V.tensor_tensor(vec[:, :, :, :CS], p01[:, q, :, 1].unsqueeze(2).broadcast_to([P, 2, 3, CS]),
                                              three(CS), ALU.mult))
                        s.did(V.tensor_tensor(row[:, :, :CS], p01[:, q, :, 0], one(0, CS), ALU.mult))
                        s.after(d)
                        s.did(V.tensor_tensor(vec[:, :, :, CS:], e1, w2y[:, q].unsqueeze(2).broadcast_to([P, 2, 3, CV]), ALU.mult))
                        s.did(V.tensor_tensor(scal1, w[:, :, 160:192], dot[:, q], ALU.mult))
                        s.did(V.tensor_copy(row[:, :, T0I], tabs[:, 1, bass.ds(2 * (K * i + k), 2)]))
                        s.did(V.tensor_copy(carry[:, q], tabs[:, 2, bass.ds(2 * (K * i + k), 2)]))
                        s.after(s.n)
                        V.memset(row[:, :, T0W - 2:T0W - 1], 1.0).then_inc(mid_done, 1)
                    assert s.n == K * PER, s.n


def load_pair(sp, v, rec, es, loaded, ids_read, es_read, y_read, i, k):
    slot, use = k % K, i + k // K
    if not isinstance(use, int) or use > 0:
        wait_alone(sp, ids_read[slot], 32 * use)
    wait_alone(sp, es_read, START + K * i + k - K + 1)
    wait_alone(sp, y_read, START + K * i + k - K + 1)
    sp.dma_start(rec[:, slot, :], v["meta"][bass.ds(K * i + k, 1)].rearrange("o p w -> (o p) w")).then_inc(loaded[slot], 16)
    sp.dma_start(es[:FC, slot, :], v["esT"][:, bass.ds(256 * (K * i + k), 256)]).then_inc(loaded[slot], 16)


def sum_segments(nc, pe, onehot, vals, carry, acc, sums, width, kept, sum_done, i, k):
    q = k % 2
    for j in range(2):
        slot = 2 * q + j
        pe.wait_ge(kept, START + 2 * (K * i + k) + j - 1)
        nc.tensor.matmul(sums[:, j, :width], onehot[:, q, j, :], vals[:, q, j, :], start=True, stop=True)
        pe.wait_ge(kept, START + 2 * (K * i + k) + j)
        nc.tensor.matmul(sums[:1, j, :width], carry[:, q, j:j + 1], acc[:, (slot - 1) % K, :width],
                         start=False, stop=True, skip_group_check=True).then_inc(sum_done, 1)


def keep_sums(nc, act, sums, acc, rows, width, rowidx, sum_done, kept, scattered, i, k):
    for j in range(2):
        slot = 2 * (k % 2) + j
        act.wait_ge(sum_done, START + 2 * (K * i + k) + j + 1)
        if not isinstance(i, int) or k >= 2:
            act.wait_ge(scattered[slot], 16 * (2 * i + k // 2))
        nc.scalar.activation(rowidx[:, bass.ds(2 * (K * i + k) + j, 1)], sums[:, j, width - 1:width], ACT.Copy, bias=float(SKIP))
        nc.scalar.activation(rows[:, slot:slot + 1], sums[:, j, width - 1:width], ACT.Copy, bias=float(SKIP))
        nc.scalar.activation(acc[:, slot, :width], sums[:, j, :width], ACT.Copy).then_inc(kept, 1)


def scatter(nc, pool, table, acc, rows, width, kept, scattered, i, k):
    for j in range(2):
        slot = 2 * (k % 2) + j
        wait_alone(pool, kept, START + 2 * (K * i + k) + j + 1)
        nc.gpsimd.indirect_dma_start(table, bass.IndirectOffsetOnAxis(ap=rows[:, slot:slot + 1], axis=0),
                                     acc[:, slot, :width], None, bounds_check=N - 1, oob_is_err=False).then_inc(scattered[slot], 16)


def scatter_end(pool, scattered):
    for s in scattered:
        pool.wait_ge(s, 16 * (NT // K))


def layer_norm(V, s, act_root, stats, mv, var, rstd, row, j2, width=D):
    for j in range(j2):
        s.did(V.bn_stats(stats[:, j, :], row[:, j, :width]))
    s.after_alone(s.n)
    for j in range(j2):
        s.did(V.bn_aggr(mv[:, j, :], stats[:, j, :]))
    s.after(s.n)
    act_root(V.tensor_scalar(var[:, :], mv[:, :, 1], EPS, None, ALU.add))


def nodes1(nc, v):
    W, ident = v["W"], v["ident"]
    x3, t3, x13, a3, b3 = (node_pairs(v[k]) for k in ("x", "T0", "X1", "A", "B"))
    with Stage(nc, "nodes1") as st:
        xs, ts = st.sb("xs", [P, 2, 2, D]), st.sb("ts", [P, 2, 2, T0W])
        xT, tT = st.sb("xT", [P, 2, 256]), st.sb("tT", [P, 2, 512])
        nT = st.sb("nT", [P, 2, 256])
        per = st.sb("per", [P, 4, 2])
        ya, yb, x1 = st.sb("ya", [P, 2, D]), st.sb("yb", [P, 2, D]), st.sb("x1", [P, 2, D])
        sq, norm, norm2 = st.sb("sq", [P, 2, 96]), st.sb("norm", [P, 2, D]), st.sb("norm2", [P, 2, D])
        stats, mv = st.sb("stats", [P, 2, 6]), st.sb("mv", [P, 2, 2])
        var, root, rstd = (st.sb(n, [P, 2]) for n in ("var", "root", "rstd"))
        var2, root2, rstd2 = (st.sb(n, [P, 2, 2]) for n in ("var2", "root2", "rstd2"))
        ab = st.sb("ab", [P, 2, 2 * DX])
        tp, cp = st.ps("tp", [P, 2, 512]), st.ps("cp", [P, 2, 512])
        xp, abp = st.ps("xp", [P, 2, 256]), st.ps("abp", [P, 2, 512])
        loaded = [st.sem(f"loaded{g}") for g in range(2)]
        sem = {n: st.sem(n) for n in ("turned", "kept", "conv", "varied", "rooted", "x1_done", "norm_done",
                                      "turned2", "kept2", "ab_done", "ab_kept", "x1_stored", "ab_stored", "step")}
        with nc.Block() as block:

            @block.sync
            def _(sp):
                sp.sem_inc(sem["x1_stored"], START)
                sp.sem_inc(sem["ab_stored"], START)

                def load(m, g):
                    sp.dma_start(ts[:, g], pair_at(t3, m)).then_inc(loaded[g], 16)
                    sp.dma_start(xs[:, g], pair_at(x3, m)).then_inc(loaded[g], 16)

                def store_x1(m):
                    sp.wait_ge(sem["x1_done"], m + 1)
                    sp.dma_start(pair_at(x13, m), x1[:, :, :]).then_inc(sem["x1_stored"], 16)

                def store_ab(m):
                    sp.wait_ge(sem["ab_kept"], START + m + 1)
                    sp.dma_start(pair_at(a3, m), ab[:, :, :DX]).then_inc(sem["ab_stored"], 16)
                    sp.dma_start(pair_at(b3, m), ab[:, :, DX:]).then_inc(sem["ab_stored"], 16)

                load(0, 0)
                load(1, 1)
                store_x1(0)
                load(2, 0)
                with sp.Fori(0, (NB - 3) // 2) as h:
                    for g in range(2):
                        store_x1(2 * h + g + 1)
                        load(2 * h + g + 3, 1 - g)
                        store_ab(2 * h + g)
                for m in range(NB - 2, NB):
                    store_x1(m)
                    store_ab(m - 1)
                store_ab(NB - 1)
                sp.wait_ge(sem["x1_stored"], START + 16 * NB)
                sp.wait_ge(sem["ab_stored"], START + 32 * NB)

            @block.tensor
            def _(pe):
                T = nc.tensor
                pe.sem_inc(sem["turned2"], START)

                def convolution(m, g, use):
                    pe.wait_ge(loaded[g], 32 * use + 32)
                    for j in range(2):
                        for c in range(4):
                            T.transpose(tp[:96, j, c * P:(c + 1) * P], ts[:, g, j, 96 * c:96 * c + 96], ident[:, :])
                        T.transpose(xp[:CS, j, :P], xs[:, g, j, :CS], ident[:, :])
                        last = T.transpose(xp[:96, j, P:], xs[:, g, j, CS:], ident[:, :])
                    last.then_inc(sem["turned"], 1)
                    pe.wait_ge(sem["kept"], m + 1)
                    if not isinstance(m, int):
                        pe.wait_ge(sem["varied"], 2 * m - 1)
                    for j in range(2):
                        T.matmul(cp[:, j, :CS], tT[:96, j, :P], W("l2s")[:, :CS], start=True, stop=True)
                        T.matmul(cp[:, j, D:D + 1], tT[:96, j, :P], W("l2s")[:, CS:CS + 1], start=True, stop=True)
                        for x in range(3):
                            T.matmul(cp[:, j, CS + x:D:3], tT[:96, j, (x + 1) * P:(x + 2) * P], W("l2v"), start=True, stop=True)
                        T.matmul(cp[:, j, 164:164 + CS], xT[:CS, j, :P], W("sc0"), start=True, stop=True)
                        last = T.matmul(cp[:, j, 164 + CS:164 + D], xT[:96, j, P:], W("sc1"), start=True, stop=True)
                    last.then_inc(sem["conv"], 1)

                def projections(m):
                    wait_alone(pe, sem["norm_done"], m + 1)
                    for j in range(2):
                        T.transpose(xp[:CS, j, :P], norm[:, j, :CS], ident[:, :])
                        last = T.transpose(xp[:96, j, P:], norm2[:, j, CS:], ident[:, :])
                    last.then_inc(sem["turned2"], 1)
                    pe.wait_ge(sem["kept2"], m + 1)
                    pe.wait_ge(sem["ab_kept"], START + m)
                    for j in range(2):
                        for o, s_, v_ in ((0, "ws_src", "wv_src"), (DX, "ws_dst", "wv_dst")):
                            T.matmul(abp[:, j, o:o + CS], nT[:CS, j, :P], W(s_), start=True, stop=True)
                            last = T.matmul(abp[:, j, o + CS:o + DX], nT[:96, j, P:], W(v_), start=True, stop=True)
                    last.then_inc(sem["ab_done"], 1)

                convolution(0, 0, 0)
                with pe.Fori(0, NB // 2) as h:
                    for g in range(2):
                        convolution(2 * h + g + 1, 1 - g, h + g)
                        projections(2 * h + g)
                projections(NB - 1)

            @block.scalar
            def _(act):
                S = nc.scalar
                act.sem_inc(sem["ab_kept"], START)

                def keep(m):
                    act.wait_ge(sem["turned"], m + 1)
                    if not isinstance(m, int):
                        act.wait_ge(sem["conv"], m)
                    S.activation(tT[:96, :, :], tp[:96, :, :], ACT.Copy)
                    S.activation(xT[:CS, :, :P], xp[:CS, :, :P], ACT.Copy)
                    S.activation(xT[:96, :, P:], xp[:96, :, P:], ACT.Copy).then_inc(sem["kept"], 1)

                def roots(m):
                    act.wait_ge(sem["varied"], 2 * m + 1)
                    S.activation(root[:, :], var[:, :], ACT.Sqrt).then_inc(sem["rooted"], 1)
                    act.wait_ge(sem["varied"], 2 * m + 2)
                    S.activation(root2[:, :, :], var2[:, :, :], ACT.Sqrt).then_inc(sem["rooted"], 1)

                def keep_projections(m):
                    act.wait_ge(sem["turned2"], START + m + 1)
                    S.activation(nT[:CS, :, :P], xp[:CS, :, :P], ACT.Copy)
                    S.activation(nT[:96, :, P:], xp[:96, :, P:], ACT.Copy).then_inc(sem["kept2"], 1)
                    act.wait_ge(sem["ab_done"], m + 1)
                    act.wait_ge(sem["ab_stored"], START + 32 * m)
                    S.activation(ab[:, :, :], abp[:, :, :2 * DX], ACT.Copy).then_inc(sem["ab_kept"], 1)

                keep(0)
                roots(0)
                with act.Fori(0, NB - 1) as b:
                    keep(b + 1)
                    keep_projections(b)
                    roots(b + 1)
                keep_projections(NB - 1)

            @block.vector
            def _(dve):
                V = nc.vector
                s = Steps(dve, sem["step"])
                PER = 29

                def body(m, g, use):
                    s.n, s.base = 0, PER * m

                    def rooted(ins, n):
                        ins.then_inc(sem["varied"], 1)
                        dve.wait_ge(sem["rooted"], 2 * m + n)

                    al, r, cnt, rc = (per[:, q, :] for q in range(4))
                    dve.wait_ge(loaded[g], 32 * use + 32)
                    s.link(V.tensor_scalar(cnt, ts[:, g, :, T0W - 2], 1.0, None, ALU.max))
                    s.link(V.reciprocal(rc, cnt))
                    s.link(V.tensor_tensor(r, rc, v["attr_s"][:, bass.ds(2 * m, 2)], ALU.mult))
                    s.link(V.tensor_tensor(cnt, r, r, ALU.mult))
                    dve.wait_ge(sem["conv"], m + 1)
                    s.did(V.tensor_tensor(al, cnt, cp[:, :, D], ALU.mult))
                    for j in range(2):
                        s.did(V.scalar_tensor_tensor(ya[:, j, :], cp[:, j, 164:164 + D], v["attr_s"][:, bass.ds(2 * m + j, 1)],
                                                     xs[:, g, j, :], ALU.mult, ALU.add))
                    s.after(s.n)
                    for j in range(2):
                        s.did(V.scalar_tensor_tensor(yb[:, j, :], cp[:, j, :D], al[:, j:j + 1], ya[:, j, :], ALU.mult, ALU.add))
                    s.after(s.n)
                    layer_norm(V, s, lambda ins: rooted(ins, 1), stats, mv, var, rstd, yb, 2)
                    s.link(V.reciprocal(rstd[:, :], root[:, :]))
                    dve.wait_ge(sem["x1_stored"], START + 16 * m)
                    for j in range(2):
                        s.did(V.tensor_scalar(x1[:, j, :], yb[:, j, :], mv[:, j, 0:1], rstd[:, j:j + 1], ALU.subtract, ALU.mult))
                    s.after(s.n)
                    V.tensor_tensor(sq[:, :, :], x1[:, :, CS:], x1[:, :, CS:], ALU.mult).then_inc(sem["x1_done"], 1)
                    for j in range(2):
                        s.did(V.bn_stats(stats[:, j, :], x1[:, j, :CS]))
                    s.after_alone(s.n)
                    for j in range(2):
                        s.did(V.bn_aggr(mv[:, j, :], stats[:, j, :]))
                    dve.wait_ge(sem["x1_done"], m + 1)
                    s.link(V.tensor_reduce(per[:, 3, :], sq[:, :, :], AX.X, ALU.add))
                    s.did(V.tensor_scalar(var2[:, 1, :], per[:, 3, :], 1.0 / CV, EPS, ALU.mult, ALU.add))
                    rooted(V.tensor_scalar(var2[:, 0, :], mv[:, :, 1], EPS, None, ALU.add), 2)
                    s.link(V.reciprocal(rstd2[:, :, :], root2[:, :, :]))
                    dve.wait_ge(sem["turned2"], START + m)
                    for j in range(2):
                        s.did(V.tensor_scalar(norm[:, j, :CS], x1[:, j, :CS], mv[:, j, 0:1], rstd2[:, 0, j:j + 1], ALU.subtract, ALU.mult))
                        s.did(V.tensor_scalar(norm[:, j, CS:], x1[:, j, CS:], rstd2[:, 1, j:j + 1], None, ALU.mult))
                    s.after(s.n)
                    s.did(V.tensor_tensor(norm2[:, :, :CS], norm[:, :, :CS], W("gamma_s").unsqueeze(1).broadcast_to([P, 2, CS]), ALU.mult))
                    s.did(V.tensor_tensor(norm2[:, :, CS:].rearrange("p j (u m) -> p j u m", m=3),
                                          norm[:, :, CS:].rearrange("p j (u m) -> p j u m", m=3),
                                          W("gamma_v").unsqueeze(1).unsqueeze(3).broadcast_to([P, 2, CV, 3]), ALU.mult))
                    s.after(s.n)
                    V.tensor_tensor(norm[:, :, :CS], norm2[:, :, :CS], W("beta_s").unsqueeze(1).broadcast_to([P, 2, CS]),
                                    ALU.add).then_inc(sem["norm_done"], 1)
                    assert s.n == PER, s.n

                with dve.Fori(0, NB // 2) as h:
                    for g in range(2):
                        body(2 * h + g, g, h)
                body(NB - 1, 0, NB // 2)


def edges1(nc, v):
    W = v["W"]
    with Stage(nc, "edges1") as st:
        rec = st.sb("rec", [P, K, META], I32)
        es = st.sb("es", [P, K, 256])
        msg = st.sb("msg", [P, K, 2, DX])
        yk = st.sb("yk", [P, K, 2, 6])
        pw = st.sb("pw", [P, 2, 2, 2, CS])
        wy = st.sb("wy", [P, 2, 2, CV])
        vy, dot = st.sb("vy", [P, 2, 2, 96]), st.sb("dot", [P, 2, 2, CV])
        ca, cb = st.sb("ca", [P, 2, 2, 96]), st.sb("cb", [P, 2, 2, 96])
        cr = st.sb("cr", [P, 2, 2, 96])
        prod1, prod2 = st.sb("prod1", [P, 2, 2, 512]), st.sb("prod2", [P, 2, 2, 512])
        pt1, pt2 = st.sb("pt1", [P, 2, 512]), st.sb("pt2", [P, 2, 512])
        a_sb = st.sb("a_sb", [P, 2, 2, CS])
        sig = st.sb("sig", [P, 2, 2, 96])
        lr, la = st.sb("lr", [P, 2, 2, CS]), st.sb("la", [P, 2, 2, CS])
        vg = st.sb("vg", [P, 2, 2, 5 * CV])
        hs = st.sb("hs", [P, K, 2, HEADS, HW + 1])
        wp, xp = st.ps("wp", [P, 2, 512]), st.ps("xp", [P, 2, 512])
        op, hp = st.ps("op", [P, 2, 2, 256]), st.ps("hp", [P, 2, 256])
        idle, idle_out = st.sb("idle", [P, 512], BF16), st.ps("idle_out", [P, 512])
        loaded = [st.sem(f"loaded{k}") for k in range(K)]
        from_src = [st.sem(f"from_src{k}") for k in range(K)]
        from_dst = [st.sem(f"from_dst{k}") for k in range(K)]
        stored = [st.sem(f"stored{k}") for k in range(K)]
        w_done, prod1_done, prod2_done = st.sem("w_done"), st.sem("prod1_done"), st.sem("prod2_done")
        turned, kept, s1_done, sig_done = st.sem("turned"), st.sem("kept"), st.sem("s1_done"), st.sem("sig_done")
        op_read, h_done, h_kept, step = st.sem("op_read"), st.sem("h_done"), st.sem("h_kept"), st.sem("step")
        ones, scal2_done, cleared = st.sem("ones"), st.sem("scal2_done"), st.sem("cleared")
        with nc.Block() as block:

            @block.sync
            def _(sp):
                load = lambda i, k: load_pair(sp, v, rec, es, loaded, from_dst, w_done, prod1_done, i, k)
                for q in stored:
                    sp.sem_inc(q, START)
                sp.wait_ge(cleared, 1)
                for k in range(K):
                    load(0, k)
                with sp.Fori(0, NI) as i:
                    for k in range(K):
                        load(i, k + K)
                        sp.wait_ge(h_kept, START + K * i + k + 1)
                        sp.dma_start(v["H"][bass.ds(K * i + k, 1)].rearrange("o p w -> (o p) w"),
                                     hs[:, k].rearrange("p j h w -> p (j h w)")).then_inc(stored[k], 16)
                for k in range(K):
                    sp.wait_ge(stored[k], START + 16 * NI)
                    sp.wait_ge(loaded[k], 32 * (NPL // K))

            @block.gpsimd
            def _(pool):
                def source(i, k):
                    slot, use = k % K, i + k // K
                    wait_alone(pool, loaded[slot], 32 * use + 32)
                    wait_alone(pool, prod1_done, START + K * i + k - K + 1)
                    for j in range(2):
                        nc.gpsimd.indirect_dma_start(msg[:, slot, j, :], None, v["A"], bass.IndirectOffsetOnAxis(
                            ap=rec[:, slot, j:j + 1], axis=0)).then_inc(from_src[slot], 16)

                def destination(i, k):
                    slot, use = k % K, i + k // K
                    wait_alone(pool, from_src[slot], 32 * use + 32)
                    for j in range(2):
                        nc.gpsimd.indirect_dma_start(msg[:, slot, j, :], None, v["B"], bass.IndirectOffsetOnAxis(
                            ap=rec[:, slot, 2 + j:3 + j], axis=0), compute_op=ALU.add).then_inc(from_dst[slot], 16)

                source(0, 0)
                with pool.Fori(0, NI) as i:
                    for k in range(K):
                        destination(i, k)
                        source(i, k + 1)
                destination(NI, 0)
                source(NI, 1)
                destination(NI, 1)

            @block.scalar
            def _(act):
                S = nc.scalar
                for q in (kept, sig_done, h_kept, scal2_done):
                    act.sem_inc(q, START)

                def keep(pt, u):
                    for j in range(2):
                        act.wait_ge(turned, START + u + j + 1)
                        S.activation(pt[:, j, :], xp[:, j, :], ACT.Copy).then_inc(kept, 1)

                def sigmoids(i, k):
                    q = k % 2
                    act.wait_ge(s1_done, START + K * i + k + 1)
                    act.wait_ge(prod2_done, START + K * i + k - 1)
                    S.activation(a_sb[:, q], op[:, q, :, :CS], ACT.Copy)
                    S.activation(sig[:, q], op[:, q, :, CS:160], ACT.Sigmoid).then_inc(sig_done, 1)

                def scalar_terms(i, k):
                    q = k % 2
                    act.wait_ge(sig_done, START + K * i + k + 1)
                    act.wait_ge(turned, START + 4 * (K * i + k) - 2)
                    for j in range(2):
                        for m in range(4):
                            at = 384 if m == 0 else P * (m - 1)
                            last = S.activation(prod2[:, q, j, at:at + CS], sig[:, q, j, :CS], ACT.Copy,
                                                scale=yk[:, k % K, j, m:m + 1])
                    last.then_inc(scal2_done, 1)

                keep(pt1, 0)
                act.wait_ge(ones, 1)
                sigmoids(0, 0)
                scalar_terms(0, 0)
                keep(pt1, 2)
                sigmoids(0, 1)
                with act.Fori(0, NI) as i:
                    for k in range(K):
                        u = 4 * (K * i + k) + 4
                        keep(pt2, u)
                        scalar_terms(i, k + 1)
                        act.wait_ge(h_done, START + K * i + k + 1)
                        act.wait_ge(stored[k], START + 16 * i)
                        S.activation(hs[:, k, :, :, :HW], hp[:, :, :D].rearrange("p j (h w) -> p j h w", h=HEADS),
                                     ACT.Copy).then_inc(h_kept, 1)
                        keep(pt1, u + 2)
                        sigmoids(i, k + 2)

            @block.tensor
            def _(pe):
                T = nc.tensor
                for q in (w_done, turned, s1_done, h_done):
                    pe.sem_inc(q, START)

                def keep_warm(n):
                    for _ in range(n):
                        T.matmul(idle_out[:, :], idle[:, :P], idle[:, :], start=True, stop=True)

                def weights(i, k):
                    slot = k % K
                    pe.wait_ge(loaded[slot], 32 * (i + k // K) + 32)
                    pe.wait_ge(prod1_done, START + K * i + k - 1)
                    for j in range(2):
                        last = T.matmul(wp[:, k % 2, j * WN1:(j + 1) * WN1], es[:, slot, j * P:(j + 1) * P], W("w_rbf"),
                                        start=True, stop=True)
                    last.then_inc(w_done, 1)

                def turn(prod, u):
                    for j in range(2):
                        pe.wait_ge(kept, START + u + j - 1)
                        for c in range(4):
                            last = T.transpose(xp[:, j, c * P:(c + 1) * P], prod[:, j, c * P:(c + 1) * P], v["ident"][:, :])
                        last.then_inc(turned, 1)

                def stage1(i, k, u):
                    q = k % 2
                    pe.wait_ge(op_read, START + K * i + k - 1)
                    for j in range(2):
                        pe.wait_ge(kept, START + u + j + 1)
                        T.matmul(op[:, q, j, :160], pt1[:, j, 384:], v["w1s"][:, :], start=True, stop=True)
                        for x in range(3):
                            last = T.matmul(op[:, q, j, 160 + CV * x:192 + CV * x], pt1[:, j, x * P:(x + 1) * P], v["w1v"][:, :],
                                            start=True, stop=True)
                    last.then_inc(s1_done, 1)

                pe.wait_ge(ones, 1)
                weights(0, 0)
                weights(0, 1)
                for k in range(2):
                    pe.wait_ge(prod1_done, START + k + 1)
                    turn(prod1[:, k], 2 * k)
                    stage1(0, k, 2 * k)
                    if k == 0:
                        weights(0, 2)
                with pe.Fori(0, NI) as i:
                    for k in range(K):
                        u = 4 * (K * i + k) + 4
                        pe.wait_ge(prod2_done, START + K * i + k + 1)
                        pe.wait_ge(scal2_done, START + K * i + k + 1)
                        turn(prod2[:, k % 2], u)
                        keep_warm(1)
                        weights(i, k + 3)
                        pe.wait_ge(h_kept, START + K * i + k)
                        for j in range(2):
                            pe.wait_ge(kept, START + u + j + 1)
                            heads = hp[:, j, :D].rearrange("p (h w) -> p h w", h=HEADS)
                            T.matmul(heads[:, :, :AS], pt2[:, j, 384:], v["w2s"][:, :], start=True, stop=True)
                            for x in range(3):
                                last = T.matmul(heads[:, :, AS + AV * x:AS + AV * x + AV], pt2[:, j, x * P:(x + 1) * P], v["w2v"][:, :],
                                                start=True, stop=True)
                        last.then_inc(h_done, 1)
                        keep_warm(1)
                        pe.wait_ge(prod1_done, START + K * i + k + 3)
                        turn(prod1[:, k % 2], u + 2)
                        keep_warm(1)
                        stage1(i, k + 2, u + 2)

            @block.vector
            def _(dve):
                V = nc.vector
                for q in (prod1_done, prod2_done, op_read):
                    dve.sem_inc(q, START)
                V.memset(es[:, :, :], 0.0).then_inc(cleared, 1)
                s = Steps(dve, step)
                s.did(V.memset(prod1[:, :, :, 480:], 0.0))
                s.did(V.memset(prod2[:, :, :, 480:], 0.0))
                s.did(V.memset(idle[:, :], 1.0))
                s.link(V.memset(hs[:, :, :, :, HW:], 1.0))
                dve.sem_inc(ones, 1)
                PER = 21

                three = lambda ap: ap.rearrange("p j (m u) -> p j m u", m=3)
                over = lambda ap, m: ap.unsqueeze(2).broadcast_to([P, 2, m, ap.shape[-1]])
                blocks = lambda out: out[:, :, :384].rearrange("p j (m w) -> p j m w", m=3)
                by = lambda y, a, n: y[:, :, a:a + 3].unsqueeze(3).broadcast_to([P, 2, 3, n])

                def layer1(i, k):
                    slot, q = k % K, k % 2
                    y = rec[:, slot, 4:].bitcast(F32).rearrange("p (j c) -> p j c", j=2)
                    m, out = msg[:, slot], prod1[:, q]
                    w = wp[:, q, :2 * WN1].rearrange("p (j w) -> p j w", j=2)
                    dve.wait_ge(from_dst[slot], 32 * (i + k // K) + 32)
                    a = s.did(V.tensor_tensor(three(vy[:, 0]), three(m[:, :, CS:D]), by(y, 1, CV), ALU.mult))
                    b = s.did(V.tensor_tensor(three(ca[:, 0]), three(m[:, :, CS + CV:CS + 4 * CV]), by(y, 3, CV), ALU.mult))
                    b = s.did(V.tensor_tensor(three(cb[:, 0]), three(m[:, :, CS + 2 * CV:]), by(y, 2, CV), ALU.mult))
                    s.after(a)
                    a = s.did(V.tensor_reduce(dot[:, 0], vy[:, 0].rearrange("p j (m u) -> p j u m", m=3), AX.X, ALU.add))
                    s.did(V.tensor_copy(yk[:, slot], y))
                    s.after(b)
                    b = s.did(V.tensor_tensor(cr[:, 0], ca[:, 0], cb[:, 0], ALU.subtract))
                    dve.wait_ge(w_done, START + K * i + k + 1)
                    c = s.did(V.tensor_tensor(wy[:, q], w[:, :, 128:160], y[:, :, 0:1].broadcast_to([P, 2, CV]), ALU.mult))
                    d = s.did(V.tensor_tensor(pw[:, q], w[:, :, :2 * CS].rearrange("p j (a u) -> p j a u", a=2),
                                              over(m[:, :, :CS], 2), ALU.mult))
                    dve.wait_ge(turned, START + 4 * (K * i + k) - 8)
                    s.after(b)
                    s.did(V.tensor_tensor(blocks(out)[:, :, :, 96:], three(cr[:, 0]), over(w[:, :, 192:], 3), ALU.mult))
                    s.did(V.tensor_tensor(out[:, :, 448:480], dot[:, 0], w[:, :, 160:192], ALU.mult))
                    s.after(d)
                    s.did(V.tensor_tensor(blocks(out)[:, :, :, CS:96], three(m[:, :, CS:D]), over(wy[:, q], 3), ALU.mult))
                    s.did(V.tensor_tensor(out[:, :, 384:448], pw[:, q, :, 0], y[:, :, 0:1].broadcast_to([P, 2, CS]), ALU.mult))
                    V.tensor_tensor(blocks(out)[:, :, :, :CS], over(pw[:, q, :, 1], 3), by(y, 1, CS), ALU.mult).then_inc(prod1_done, 1)

                def layer2(i, k):
                    slot, q = k % K, k % 2
                    y, out = yk[:, slot], prod2[:, q]
                    dve.wait_ge(sig_done, START + K * i + k + 1)
                    a = s.did(V.tensor_tensor(three(vg[:, q, :, :96]), three(op[:, q, :, 160:]), over(sig[:, q, :, CS:], 3), ALU.mult))
                    V.scalar_tensor_tensor(lr[:, q], op[:, q, :, :CS], 0.2, a_sb[:, q], ALU.mult, ALU.max).then_inc(op_read, 1)
                    dve.wait_ge(turned, START + 4 * (K * i + k) - 2)
                    s.after(a)
                    d = s.did(V.tensor_copy(vg[:, q, :, 96:], vg[:, q, :, :2 * CV]))
                    a = s.did(V.tensor_tensor(three(vy[:, 1]), three(vg[:, q, :, :96]), by(y, 1, CV), ALU.mult))
                    dve.wait_ge(op_read, START + K * i + k + 1)
                    b = s.did(V.tensor_tensor(la[:, q], lr[:, q], W("alpha_dot").unsqueeze(1).broadcast_to([P, 2, CS]), ALU.mult))
                    s.after(d)
                    s.did(V.tensor_tensor(three(ca[:, 1]), three(vg[:, q, :, CV:4 * CV]), by(y, 3, CV), ALU.mult))
                    d = s.did(V.tensor_tensor(three(cb[:, 1]), three(vg[:, q, :, 2 * CV:]), by(y, 2, CV), ALU.mult))
                    s.did(V.tensor_tensor(blocks(out)[:, :, :, CS:96], three(vg[:, q, :, :96]),
                                          y[:, :, 0:1].unsqueeze(3).broadcast_to([P, 2, 3, CV]), ALU.mult))
                    s.after(b)
                    s.did(V.tensor_reduce(out[:, :, 448:480], vy[:, 1].rearrange("p j (m u) -> p j u m", m=3), AX.X, ALU.add))
                    s.did(V.tensor_reduce(v["logit"][:, bass.ds(2 * (K * i + k), 2), :],
                                          la[:, q].rearrange("p j (h a) -> p j h a", h=HEADS), AX.X, ALU.add))
                    s.after(d)
                    V.tensor_tensor(blocks(out)[:, :, :, 96:], three(ca[:, 1]), three(cb[:, 1]), ALU.subtract).then_inc(prod2_done, 1)

                layer1(0, 0)
                layer1(0, 1)
                first = s.n
                with dve.Fori(0, NI) as i:
                    s.n = 0
                    s.base = first + K * PER * i
                    for k in range(K):
                        layer2(i, k)
                        layer1(i, k + 2)
                    assert s.n == K * PER, s.n


def softmax(nc, v):
    ident, logit = v["ident"], v["logit"]
    seg_open, seg_shut = v["seg_open"], v["seg_shut"]
    with Stage(nc, "softmax") as st:
        a = st.sb("a", [P, NC, HEADS, P])
        f = st.sb("f", [P, NC, HEADS, P])
        cols = st.sb("cols", [P, 4, NC, HEADS])
        lines = st.sb("lines", [HEADS, 4, NTC])
        block_ = st.sb("block", [HEADS, 2, NTC])
        run = st.sb("run", [HEADS, 2, NTC])
        given = block_
        back = st.sb("back", [P, 2, NC, HEADS])
        tp = st.ps("tp", [P, 2, 512])
        cp = st.ps("cp", [HEADS, 2, 512])
        bp = st.ps("bp", [P, 2, NC, HEADS])
        turned, kept, tails, cturned, ckept = (st.sem(n) for n in ("turned", "kept", "tails", "cturned", "ckept"))
        carried, bturned, bkept, lowered = (st.sem(n) for n in ("carried", "bturned", "bkept", "lowered"))
        exped, step = st.sem("exped"), st.sem("step")
        back_turned, written = st.sem("back_turned"), st.sem("written")
        groups = [(q, g) for q in range(4) for g in range(0, NC, 4)]
        width = lambda g: min(4, NC - g)
        with nc.Block() as block:

            @block.tensor
            def _(pe):
                T = nc.tensor
                for c in range(NC):
                    if c >= 2:
                        pe.wait_ge(kept, c - 1)
                    for h in range(HEADS):
                        last = T.transpose(tp[:, c % 2, h * P:(h + 1) * P], logit[:, c * P:(c + 1) * P, h], ident[:, :])
                    last.then_inc(turned, 1)
                pe.wait_ge(tails, 1)
                for n, (q, g) in enumerate(groups):
                    if n >= 2:
                        pe.wait_ge(ckept, n - 1)
                    for c in range(width(g)):
                        last = T.transpose(cp[:, n % 2, c * P:(c + 1) * P], cols[:, q, g + c, :], ident[:, :])
                    last.then_inc(cturned, 1)
                pe.wait_ge(carried, 1)
                for q in range(2):
                    for c in range(NC):
                        last = T.transpose(bp[:, q, c, :], given[:, q, c * P:(c + 1) * P], ident[:HEADS, :HEADS])
                last.then_inc(bturned, 1)
                for c in range(NC):
                    pe.wait_ge(exped, c + 1)
                    if c >= 2:
                        pe.wait_ge(written, c - 1)
                    for h in range(HEADS):
                        last = T.transpose(tp[:, c % 2, h * P:(h + 1) * P], a[:, c, h, :], ident[:, :])
                    last.then_inc(back_turned, 1)

            @block.scalar
            def _(act):
                S = nc.scalar
                for c in range(NC):
                    act.wait_ge(turned, c + 1)
                    S.activation(a[:, c].rearrange("p h e -> p (h e)"), tp[:, c % 2, :], ACT.Copy).then_inc(kept, 1)
                for n, (q, g) in enumerate(groups):
                    act.wait_ge(cturned, n + 1)
                    S.activation(lines[:, q, g * P:(g + width(g)) * P], cp[:, n % 2, :width(g) * P], ACT.Copy).then_inc(ckept, 1)
                act.wait_ge(bturned, 1)
                S.activation(back[:, :, :, :], bp[:, :, :, :], ACT.Copy).then_inc(bkept, 1)
                for c in range(NC):
                    act.wait_ge(lowered, c + 1)
                    S.activation(a[:, c], f[:, c], ACT.Exp).then_inc(exped, 1)
                for c in range(NC):
                    act.wait_ge(back_turned, c + 1)
                    S.activation(logit[:, c * P:(c + 1) * P, :].rearrange("p t h -> p h t"),
                                 tp[:, c % 2, :].rearrange("p (h t) -> p h t", h=HEADS), ACT.Copy).then_inc(written, 1)
                act.wait_ge(written, NC)

            @block.vector
            def _(dve):
                V = nc.vector
                s = Steps(dve, step)
                peak = logit[:, :, :].rearrange("p t h -> p (t h)").rearrange("p (c h e) -> p c h e", c=NC, h=HEADS)
                for c in range(NC):
                    dve.wait_ge(kept, c + 1)
                    for h in range(HEADS):
                        s.did(V.tensor_tensor_scan(f[:, c, h], seg_open[:, c], a[:, c, h], -BIG, ALU.add, ALU.max))
                s.after(s.n)
                for c in range(NC):
                    for h in range(HEADS):
                        s.did(V.tensor_tensor_scan(peak[:, c, h, ::-1], seg_shut[:, c, ::-1], f[:, c, h, ::-1], -BIG, ALU.add, ALU.max))
                s.after(s.n)
                s.did(V.tensor_copy(cols[:, 0], f[:, :, :, P - 1]))
                s.did(V.tensor_copy(cols[:, 1], peak[:, :, :, 0]))
                s.did(V.tensor_copy(cols[:, 2], v["one_seg"][:, :, :]))
                s.after(s.n)
                V.tensor_copy(cols[:, 3], v["goes_on"][:, :, :]).then_inc(tails, 1)
                dve.wait_ge(ckept, len(groups))
                tail, head, one, on = (lines[:, q] for q in range(4))
                ahead, behind = block_[:, 0], block_[:, 1]
                s.did(V.memset(block_[:, 1, NTC - 1:], 0.0))
                s.did(V.tensor_tensor(ahead, one, on, ALU.mult))
                s.link(V.tensor_tensor(behind[:, :NTC - 1], one[:, :NTC - 1], on[:, 1:], ALU.mult))
                s.link(V.tensor_scalar(block_[:, :, :], block_[:, :, :], 1.0, BIG, ALU.subtract, ALU.mult))
                s.did(V.tensor_tensor_scan(run[:, 0], ahead, tail, -BIG, ALU.add, ALU.max))
                s.did(V.tensor_tensor_scan(run[:, 1, ::-1], behind[:, ::-1], head[:, ::-1], -BIG, ALU.add, ALU.max))
                s.after(s.n)
                s.did(V.memset(given[:, 0, 0:1], -BIG))
                s.did(V.memset(given[:, 1, NTC - 1:], -BIG))
                s.link(V.tensor_scalar(lines[:, 2], on, 1.0, BIG, ALU.subtract, ALU.mult))
                s.did(V.tensor_tensor(given[:, 0, 1:], run[:, 0, :NTC - 1], lines[:, 2, 1:], ALU.add))
                s.after(s.n)
                V.tensor_tensor(given[:, 1, :NTC - 1], run[:, 1, 1:], lines[:, 2, 1:], ALU.add).then_inc(carried, 1)
                dve.wait_ge(bkept, 1)
                for c in range(NC):
                    for h in range(HEADS):
                        s.did(V.scalar_tensor_tensor(f[:, c, h], v["not_first"][:, c], back[:, 0, c, h:h + 1], peak[:, c, h],
                                                     ALU.add, ALU.max))
                    s.after(s.n)
                    for h in range(HEADS):
                        s.did(V.scalar_tensor_tensor(peak[:, c, h], v["not_last"][:, c], back[:, 1, c, h:h + 1], f[:, c, h],
                                                     ALU.add, ALU.max))
                    s.after(s.n)
                    V.tensor_tensor(f[:, c], a[:, c], peak[:, c], ALU.subtract).then_inc(lowered, 1)


def edges2(nc, v):
    iota, tabs, rowidx = v["iota"], v["tabs"], v["rowidx"]
    with Stage(nc, "edges2") as st:
        hs = st.sb("hs", [P, K, 2 * HR])
        vals = st.sb("vals", [P, 2, 2, HR])
        onehot = st.sb("onehot", [P, 2, 2, P])
        carry = st.sb("carry", [P, 2, 2])
        acc = st.sb("acc", [P, K, HR])
        rows = st.sb("rows", [P, K], I32)
        sums = st.ps("sums", [P, 2, 512])
        loaded = [st.sem(f"loaded{k}") for k in range(K)]
        scattered = [st.sem(f"scattered{k}") for k in range(K)]
        vals_done, sum_done, kept, step = (st.sem(n) for n in ("vals_done", "sum_done", "kept", "step"))
        cleared = st.sem("cleared")
        with nc.Block() as block:

            @block.sync
            def _(sp):
                with sp.Fori(0, NI) as i:
                    for k in range(K):
                        sp.wait_ge(vals_done, START + K * i + k - K + 1)
                        sp.dma_start(hs[:, k, :], v["H"][bass.ds(K * i + k, 1)].rearrange("o p w -> (o p) w")).then_inc(loaded[k], 16)

            @block.gpsimd
            def _(pool):
                with pool.Fori(0, NI) as i:
                    for k in range(K):
                        scatter(nc, pool, v["T1"], acc, rows, HR, kept, scattered, i, k)
                scatter_end(pool, scattered)

            @block.scalar
            def _(act):
                act.sem_inc(kept, START)

                def keep(i):
                    for k in range(K):
                        for j in range(2):
                            slot = 2 * (k % 2) + j
                            act.wait_ge(sum_done, START + 2 * (K * i + k) + j + 1)
                            if not isinstance(i, int) or k >= 2:
                                act.wait_ge(scattered[slot], 16 * (2 * i + k // 2))
                            nc.scalar.activation(rows[:, slot:slot + 1], rowidx[:, bass.ds(2 * (K * i + k) + j, 1)], ACT.Copy)
                            nc.scalar.activation(acc[:, slot, :], sums[:, j, :HR], ACT.Copy).then_inc(kept, 1)

                keep(0)
                with act.Fori(1, NI) as i:
                    keep(i)

            @block.tensor
            def _(pe):
                pe.sem_inc(sum_done, START)
                pe.wait_ge(cleared, 1)
                with pe.Fori(0, NI) as i:
                    for k in range(K):
                        pe.wait_ge(vals_done, START + K * i + k + 1)
                        sum_segments(nc, pe, onehot, vals, carry, acc, sums, HR, kept, sum_done, i, k)

            @block.vector
            def _(dve):
                V = nc.vector
                dve.sem_inc(vals_done, START)
                V.memset(acc[:, :, :], 0.0).then_inc(cleared, 1)
                with dve.Fori(0, NI) as i:
                    for k in range(K):
                        q, n = k % 2, 2 * (K * i + k)
                        dve.wait_ge(loaded[k], 16 * i + 16)
                        dve.wait_ge(sum_done, START + 2 * (K * i + k - 2) + 2)
                        V.tensor_tensor(onehot[:, q], tabs[:, 0, bass.ds(n, 2)].unsqueeze(2).broadcast_to([P, 2, P]),
                                        iota[:, :].unsqueeze(1).broadcast_to([P, 2, P]), ALU.is_equal)
                        V.tensor_copy(carry[:, q], tabs[:, 2, bass.ds(n, 2)])
                        V.tensor_tensor(vals[:, q].rearrange("p j (h w) -> p j h w", h=HEADS),
                                        hs[:, k].rearrange("p (j h w) -> p j h w", j=2, h=HEADS),
                                        v["logit"][:, bass.ds(n, 2), :].unsqueeze(3).broadcast_to([P, 2, HEADS, HW + 1]),
                                        ALU.mult).then_inc(vals_done, 1)


def nodes2(nc, v):
    W, ident = v["W"], v["ident"]
    t3, x3, o3 = node_pairs(v["T1"]), node_pairs(v["X1"]), node_pairs(v["out"])
    with Stage(nc, "nodes2") as st:
        ts, xs = st.sb("ts", [P, 2, 2, HR]), st.sb("xs", [P, 2, 2, D])
        den, rden = st.sb("den", [P, 2, HEADS]), st.sb("rden", [P, 2, HEADS])
        agg, y, os = st.sb("agg", [P, 2, D]), st.sb("y", [P, 2, D]), st.sb("os", [P, 2, D])
        aT = st.sb("aT", [80, 2, 256])
        stats, mv = st.sb("stats", [P, 2, 6]), st.sb("mv", [P, 2, 2])
        var, root, rstd = (st.sb(n, [P, 2]) for n in ("var", "root", "rstd"))
        tp, pp = st.ps("tp", [80, 2, 256]), st.ps("pp", [P, 2, 256])
        loaded = [st.sem(f"loaded{g}") for g in range(2)]
        sem = {n: st.sem(n) for n in ("agg_done", "turned", "kept", "product", "varied", "rooted", "done", "stored", "step")}
        with nc.Block() as block:

            @block.sync
            def _(sp):
                sp.sem_inc(sem["stored"], START)

                def load(m, g):
                    sp.dma_start(ts[:, g], pair_at(t3, m)).then_inc(loaded[g], 16)
                    sp.dma_start(xs[:, g], pair_at(x3, m)).then_inc(loaded[g], 16)

                def store(m):
                    sp.wait_ge(sem["done"], START + m + 1)
                    sp.dma_start(pair_at(o3, m), os[:, :, :]).then_inc(sem["stored"], 16)

                load(0, 0)
                load(1, 1)
                with sp.Fori(0, (NB - 3) // 2) as h:
                    for g in range(2):
                        sp.wait_ge(sem["varied"], 2 * h + g + 1)
                        load(2 * h + g + 2, g)
                        store(2 * h + g)
                sp.wait_ge(sem["varied"], NB - 2)
                load(NB - 1, 0)
                for m in range(NB - 3, NB):
                    store(m)
                sp.wait_ge(sem["stored"], START + 16 * NB)

            @block.tensor
            def _(pe):
                T = nc.tensor
                pe.sem_inc(sem["turned"], START)

                def project(m):
                    pe.wait_ge(sem["agg_done"], m + 1)
                    for j in range(2):
                        for c in range(2):
                            last = T.transpose(tp[:, j, c * P:(c + 1) * P], agg[:, j, 80 * c:80 * c + 80], ident[:, :])
                    last.then_inc(sem["turned"], 1)
                    pe.wait_ge(sem["kept"], m + 1)
                    if not isinstance(m, int):
                        pe.wait_ge(sem["varied"], m)
                    for j in range(2):
                        for c in range(2):
                            last = T.matmul(pp[:, j, :D], aT[:, j, c * P:(c + 1) * P], W(f"wp{c}"), start=c == 0, stop=c == 1)
                    last.then_inc(sem["product"], 1)

                project(0)
                with pe.Fori(0, NB - 1) as b:
                    project(b + 1)

            @block.scalar
            def _(act):
                def keep(m):
                    act.wait_ge(sem["turned"], START + m + 1)
                    if not isinstance(m, int):
                        act.wait_ge(sem["product"], m)
                    nc.scalar.activation(aT[:, :, :], tp[:, :, :], ACT.Copy).then_inc(sem["kept"], 1)

                def take_root(m):
                    act.wait_ge(sem["varied"], m + 1)
                    nc.scalar.activation(root[:, :], var[:, :], ACT.Sqrt).then_inc(sem["rooted"], 1)

                keep(0)
                with act.Fori(0, NB - 1) as b:
                    keep(b + 1)
                    take_root(b)
                take_root(NB - 1)

            @block.vector
            def _(dve):
                V = nc.vector
                s = Steps(dve, sem["step"])
                dve.sem_inc(sem["done"], START)

                def divide(m, g, use):
                    dve.wait_ge(loaded[g], 32 * use + 32)
                    heads = ts[:, g].rearrange("p j (h w) -> p j h w", h=HEADS)
                    s.link(V.tensor_scalar(den[:, :, :], heads[:, :, :, HW], 1e-16, None, ALU.add))
                    s.link(V.reciprocal(rden[:, :, :], den[:, :, :]))
                    dve.wait_ge(sem["turned"], START + m)
                    V.tensor_tensor(agg[:, :, :].rearrange("p j (h w) -> p j h w", h=HEADS), heads[:, :, :, :HW],
                                    rden[:, :, :].unsqueeze(3).broadcast_to([P, 2, HEADS, HW]), ALU.mult).then_inc(sem["agg_done"], 1)

                def norm(m, g):
                    def rooted(ins):
                        ins.then_inc(sem["varied"], 1)
                        dve.wait_ge(sem["rooted"], m + 1)

                    dve.wait_ge(sem["done"], START + m)
                    dve.wait_ge(sem["product"], m + 1)
                    s.link(V.scalar_tensor_tensor(y[:, :, :], xs[:, g], 2.0, pp[:, :, :D], ALU.mult, ALU.add))
                    layer_norm(V, s, rooted, stats, mv, var, rstd, y, 2)
                    s.link(V.reciprocal(rstd[:, :], root[:, :]))
                    dve.wait_ge(sem["stored"], START + 16 * m)
                    V.tensor_scalar(os[:, 0, :], y[:, 0, :], mv[:, 0, 0:1], rstd[:, 0:1], ALU.subtract, ALU.mult)
                    V.tensor_scalar(os[:, 1, :], y[:, 1, :], mv[:, 1, 0:1], rstd[:, 1:2], ALU.subtract, ALU.mult).then_inc(sem["done"], 1)

                divide(0, 0, 0)
                first = s.n
                PER = 8
                with dve.Fori(0, NB // 2) as h:
                    s.n, s.base = 0, first + 2 * PER * h
                    for g in range(2):
                        divide(2 * h + g + 1, 1 - g, h + g)
                        norm(2 * h + g, g)
                    assert s.n == 2 * PER, s.n
                s.n, s.base = 0, first + (NB - 1) * PER
                norm(NB - 1, 0)


def weight_blocks(w):
    z = lambda *s: np.zeros(s, np.float32)
    b = {"fc1": w["Wfc1"], "fc2": w["Wfc2"], "l1_0": w["Wl1_0"], "sc0": w["Wsc0"]}
    b["l1_1"], b["sc1"] = z(96, 96), z(96, 96)
    for m in range(3):
        b["l1_1"][m::3, CV * m:CV * m + CV] = w["Wl1_1"]
        b["sc1"][m::3, m::3] = w["Wsc1"]
    b["l2s"] = np.concatenate([w["Wl2_s"], w["Wa"]], axis=1)
    b["l2v"] = w["Wl2_v"]
    b["w_rbf"] = np.concatenate([w["W_rbf"], z(P - FC, WN1)])
    for side in ("src", "dst"):
        b["ws_" + side] = w["Ws_" + side]
        b["wv_" + side] = z(96, 5 * CV)
        for m in range(5):
            b["wv_" + side][m % 3::3, CV * m:CV * m + CV] = w["Wv_" + side]
    b["wv_val"] = w["Wv_val"]
    b["w1s"] = np.concatenate([w["W_alpha"], w["Ws_val"]], axis=1)
    b["ws_valT"] = w["Ws_val"].T
    b["wg"] = w["Wg"]
    b["ws_vlin"], b["wv_vlin"] = w["Ws_vlin"], w["Wv_vlin"]
    b["w2_s"] = np.concatenate([w["w2_ss"], w["w2_vv0"]])[:, None]
    b["w2_v"] = np.concatenate([w["w2_sv"], w["w2_vs"], w["w2_vv1"]])[:, None]
    head_s = [HW * h + a for h in range(HEADS) for a in range(AS)]
    head_v = [[HW * h + AS + AV * x + a for h in range(HEADS) for a in range(AV)] for x in range(3)]
    out = z(D, D)
    out[head_s, :CS] = w["Wps"]
    for x in range(3):
        out[head_v[x], CS + x::3] = w["Wpv"]
    b["wp0"], b["wp1"] = out[:80], out[80:]
    for name, row in (("gamma_s", w["gamma_s"]), ("beta_s", w["beta_s"]), ("gamma_v", w["gamma_v"]), ("alpha_dot", w["alpha_dot"].reshape(-1))):
        b[name] = np.broadcast_to(row, (P, row.shape[0]))
    return b


def constant_columns():
    c = np.ones((P, 3), np.float32)
    c[:, 0] = 96 ** -0.5
    c[CS:96, 0] /= 3 ** 0.5
    c[96:, 1] = 2 ** -0.5
    c[CS:96, 2] = 3 ** -0.5
    return c


def kernel(**inputs):
    import numpy as _np
    import concourse.bacc as _bacc
    from concourse import mybir as _mybir
    from concourse.bass_utils import run_bass_kernel_spmd as _run

    g = {k: _np.asarray(a) for k, a in inputs.items()}
    w = {k[7:]: a for k, a in g.items() if k.startswith("L")}
    x = _np.zeros((NN, D), _np.float32)
    x[:N] = g["x"]
    attr = _np.zeros((NN,), _np.float32)
    attr[:N] = g["node_vec1"][:, 0]
    edges = NPL * 2 * P
    src, dst = _np.zeros(edges, _np.int32), _np.full(edges, N, _np.int32)
    src[:E], dst[:E] = g["src"], g["dst"]
    dstp = _np.full(P + 1 + NTC * P + P + 1, N, _np.int32)
    dstp[:P + 1] = -1
    dstp[P + 1:P + 1 + E] = g["dst"]
    es = _np.zeros((FC, edges), _np.float32)
    es[:, :E] = g["edge_attr_16"].T
    sh = _np.zeros((edges, 6), _np.float32)
    sh[:E] = g["edge_attr_4"][:, [0, 1, 2, 3, 1, 2]]
    by_pair = lambda a: a.reshape(NPL, 2, P, -1).transpose(0, 2, 1, 3).reshape(NPL, P, -1)
    meta = _np.concatenate([by_pair(src), by_pair(dst), by_pair(sh.view(_np.int32))], axis=2)
    blocks = weight_blocks(w)
    at = 0
    for name, a in blocks.items():
        W_COLS[name] = (at, a.shape[0], a.shape[1])
        at += a.shape[1]
    wpack = _np.zeros((P, at), _np.float32)
    for name, a in blocks.items():
        o, r, c = W_COLS[name]
        wpack[:r, o:o + c] = a
    ins = {"x": x, "attr": _np.ascontiguousarray(attr.reshape(2 * NB, P).T), "meta": _np.ascontiguousarray(meta),
           "dstp": dstp, "esT": es, "wpack": wpack, "wconst": constant_columns()}
    nc = _bacc.Bacc("TRN2", target_bir_lowering=False, num_devices=1)
    arrays = {f"in_{n}": a for n, a in ins.items()}
    aps = {n: nc.dram_tensor(f"in_{n}", a.shape, _mybir.dt.from_np(a.dtype), kind="ExternalInput").ap() for n, a in ins.items()}
    aps["out"] = nc.dram_tensor("out_nodes", (NN, D), _mybir.dt.float32, kind="ExternalOutput").ap()
    build(nc, **aps)
    r = _run(nc, [arrays], core_ids=[0])
    return r.results[0]["out_nodes"][:N]
```
